# Optimizing a Trainium2 kernel written in Bass

```python
import numpy as np
import jax
import jax.numpy as jnp

def _softmax(x, axis=-1):
    return jax.nn.softmax(x, axis=axis)

def _gelu(x):
    return jax.nn.gelu(x, approximate=True)

def _silu(x):
    return jax.nn.silu(x)

def _sigmoid(x):
    return jax.nn.sigmoid(x)

def _layernorm(x, axis=-1, eps=1e-05):
    m = jnp.mean(x, axis=axis, keepdims=True)
    v = jnp.var(x, axis=axis, keepdims=True)
    return (x - m) / jnp.sqrt(v + eps)

def _scatter_add(tgt, idx, src, axis=0):
    return tgt.at[idx].add(src)

def _segment_sum(src, seg, n):
    return jax.ops.segment_sum(src, seg, n)
kernel_name = 'mk_seq_postln_d1_jaxref_r4_b7ea01'

def setup_inputs(seed: int=0):
    np.random.seed(seed)
    _w = jnp.asarray

    def _L0_attn_setup():
        import jax, jax.numpy as jnp
        import numpy as np
        key = jax.random.key(seed)
        k1, k2, k3 = jax.random.split(key, 3)
        B, S, D, N = (2, 512, 256, 16)
        H = D // N
        x = jax.random.normal(k1, (B, S, D), dtype=jnp.float32)
        W_qkv = jax.random.normal(k2, (N, D, 3 * H), dtype=jnp.float32) / np.sqrt(D).astype(np.float32)
        W_out = jax.random.normal(k3, (N, H, D), dtype=jnp.float32) / np.sqrt(D).astype(np.float32)
        return {'x': x, 'W_qkv': W_qkv, 'W_out': W_out}
    _L0_attn_in = _L0_attn_setup()

    def _L0_ffn_setup():
        import jax, jax.numpy as jnp
        import numpy as np
        B, S, D = (4, 512, 256)
        P = 9
        DM = D // 4
        EPS = 1e-05

        def _mix(x, mix_kernel):
            xp = jnp.pad(x, ((0, 0), (1, 1), (0, 0)))
            return mix_kernel[0] * xp[:, :-2] + mix_kernel[1] * xp[:, 1:-1] + mix_kernel[2] * xp[:, 2:]

        def _layernorm(h, gamma, beta):
            mu = jnp.mean(h, axis=-1, keepdims=True)
            var = jnp.var(h, axis=-1, keepdims=True)
            return (h - mu) * jax.lax.rsqrt(var + EPS) * gamma + beta
        key = jax.random.key(seed)
        ks = jax.random.split(key, 12)
        sc_in = 1.0 / np.sqrt(D)
        sc_mid = 1.0 / np.sqrt(DM)
        return {'x': jax.random.normal(ks[0], (B, S, D), dtype=jnp.float32), 'mix_kernel': jax.random.normal(ks[1], (3, D), dtype=jnp.float32) * 0.5, 'W1': jax.random.normal(ks[2], (P, D, DM), dtype=jnp.float32) * sc_in, 'b1': jnp.zeros((P, DM), dtype=jnp.float32), 'W2': jax.random.normal(ks[3], (P, DM, D), dtype=jnp.float32) * sc_mid, 'b2': jnp.zeros((P, D), dtype=jnp.float32), 'Wo1': jax.random.normal(ks[4], (D, DM), dtype=jnp.float32) * sc_in, 'bo1': jnp.zeros((DM,), dtype=jnp.float32), 'Wo2': jax.random.normal(ks[5], (DM, P), dtype=jnp.float32) * sc_mid, 'bo2': jnp.zeros((P,), dtype=jnp.float32), 'gamma': jnp.ones((D,), dtype=jnp.float32), 'beta': jnp.zeros((D,), dtype=jnp.float32)}
    _L0_ffn_in = _L0_ffn_setup()
    _d = {'L0_attn_x': _L0_attn_in['x'], 'L0_attn_W_qkv': _L0_attn_in['W_qkv'], 'L0_attn_W_out': _L0_attn_in['W_out'], 'L0_ffn_mix_kernel': _L0_ffn_in['mix_kernel'], 'L0_ffn_W1': _L0_ffn_in['W1'], 'L0_ffn_b1': _L0_ffn_in['b1'], 'L0_ffn_W2': _L0_ffn_in['W2'], 'L0_ffn_b2': _L0_ffn_in['b2'], 'L0_ffn_Wo1': _L0_ffn_in['Wo1'], 'L0_ffn_bo1': _L0_ffn_in['bo1'], 'L0_ffn_Wo2': _L0_ffn_in['Wo2'], 'L0_ffn_bo2': _L0_ffn_in['bo2'], 'L0_ffn_gamma': _L0_ffn_in['gamma'], 'L0_ffn_beta': _L0_ffn_in['beta']}
    _x0 = _d['L0_attn_x']
    _d['L0_attn_x'] = jax.random.normal(jax.random.fold_in(jax.random.key(seed), 1), (8, 1024, 256), dtype=_x0.dtype)
    del _x0
    return _d

def reference(L0_attn_x, L0_attn_W_qkv, L0_attn_W_out, L0_ffn_mix_kernel, L0_ffn_W1, L0_ffn_b1, L0_ffn_W2, L0_ffn_b2, L0_ffn_Wo1, L0_ffn_bo1, L0_ffn_Wo2, L0_ffn_bo2, L0_ffn_gamma, L0_ffn_beta):

    def _L0_attn_ref(x, W_qkv, W_out):
        import jax, jax.numpy as jnp
        import numpy as np
        B, S, D = x.shape
        head_dim = W_qkv.shape[-1] // 3
        qkv = jnp.einsum('bsd,ndh->bnsh', x, W_qkv)
        q, k, v = jnp.split(qkv, 3, axis=-1)
        scale = jnp.asarray(1.0 / np.sqrt(head_dim), dtype=x.dtype)
        attn = jnp.einsum('bnqh,bnkh->bnqk', q, k) * scale
        mask = jnp.asarray(-10000000000.0, dtype=x.dtype) * (1.0 - jnp.tril(jnp.ones((S, S), dtype=x.dtype)))
        attn = jax.nn.softmax(attn + mask, axis=-1)
        out = jnp.einsum('bnqk,bnkh->bnqh', attn, v)
        out = out.reshape(B, -1, S)
        return jnp.einsum('bds,nhd->bsd', out, W_out)

    def _L0_ffn_ref(x, mix_kernel, W1, b1, W2, b2, Wo1, bo1, Wo2, bo2, gamma, beta):
        import jax, jax.numpy as jnp
        import numpy as np
        B, S, D = (4, 512, 256)
        P = 9
        DM = D // 4
        EPS = 1e-05

        def _mix(x, mix_kernel):
            xp = jnp.pad(x, ((0, 0), (1, 1), (0, 0)))
            return mix_kernel[0] * xp[:, :-2] + mix_kernel[1] * xp[:, 1:-1] + mix_kernel[2] * xp[:, 2:]

        def _layernorm(h, gamma, beta):
            mu = jnp.mean(h, axis=-1, keepdims=True)
            var = jnp.var(h, axis=-1, keepdims=True)
            return (h - mu) * jax.lax.rsqrt(var + EPS) * gamma + beta
        x_mixed = _mix(x, mix_kernel)
        h = jnp.einsum('bsd,pdm->bspm', x_mixed, W1) + b1
        stacked_paths = jnp.einsum('bspm,pmd->bspd', h, W2) + b2
        scores = jnp.tanh(x_mixed @ Wo1 + bo1) @ Wo2 + bo2
        idx = jnp.argmax(scores, axis=-1)
        weights = jax.nn.one_hot(idx, P, dtype=stacked_paths.dtype)
        collapsed = jnp.einsum('bspd,bsp->bsd', stacked_paths, weights)
        return _layernorm(x + collapsed, gamma, beta)
    x = L0_attn_x
    x = _layernorm(x + _L0_attn_ref(x, L0_attn_W_qkv, L0_attn_W_out), axis=-1)
    x = _layernorm(x + _L0_ffn_ref(x, L0_ffn_mix_kernel, L0_ffn_W1, L0_ffn_b1, L0_ffn_W2, L0_ffn_b2, L0_ffn_Wo1, L0_ffn_bo1, L0_ffn_Wo2, L0_ffn_bo2, L0_ffn_gamma, L0_ffn_beta), axis=-1)
    return x

_drawn_inputs = setup_inputs


def setup_inputs(seed=0):
    import zlib

    import numpy as np

    out = dict(_drawn_inputs(seed))
    spreads = {'L0_ffn_b1': (0.0, 0.1),
     'L0_ffn_b2': (0.0, 0.1),
     'L0_ffn_bo1': (0.0, 0.1),
     'L0_ffn_bo2': (0.0, 0.1),
     'L0_ffn_gamma': (1.0, 0.2),
     'L0_ffn_beta': (0.0, 0.1)}
    factors = {}
    for name, (base, spread) in spreads.items():
        noise = np.random.default_rng([zlib.crc32(name.encode()), seed]).standard_normal(out[name].shape)
        drawn = base * np.exp(spread * noise) if base else spread * noise
        out[name] = jnp.asarray(drawn.astype(out[name].dtype))
    for name, factor in factors.items():
        out[name] = (out[name] * factor).astype(out[name].dtype)
    return out
```

```python
from contextlib import ExitStack

import concourse.bass as bass
from concourse import mybir

ALU = mybir.AluOpType
ACT = mybir.ActivationFunctionType
AX_X = mybir.AxisListType.X
F32 = mybir.dt.float32
BF16 = mybir.dt.bfloat16

P = 128
BATCH, SEQ, D = 8, 1024, 256
HEADS, HD = 16, 16
KC = D // P
TILES = SEQ // P
CHUNK = 512
CHUNKS = SEQ // CHUNK
CT = CHUNK // P
QUAD = 4
QUADS = HEADS // QUAD
SLOTS = BATCH * QUADS
PARTS = 3
TERMS = [(0, 0), (0, 1), (0, 2), (1, 0), (1, 1), (2, 0)]
TROWS = len(TERMS) * HD
MROWS = TROWS + PARTS
SCALE = 0.25
NEG = -4.0e10
VW = 2 * HD


def identity(eng, tile, done):
    eng.memset(tile[:, :], 0.0).then_inc(done, 1)
    eng.wait_ge(done, 1)
    eng.affine_select(out=tile[:, :], in_=tile[:, :], compare_op=ALU.not_equal, fill=1.0,
                      base=0, pattern=[[-1, P]], channel_multiplier=1).then_inc(done, 1)


def project(nc, x, w_qkv, qk_parts, v_rows):
    with ExitStack() as ctx:
        def sb(name, shape, dt):
            return ctx.enter_context(nc.sbuf_tensor(name, shape, dt))

        def pb(name, shape, dt):
            return ctx.enter_context(nc.psum_tensor(name, shape, dt))

        def sem(name):
            return ctx.enter_context(nc.semaphore(name))

        QKM = 2 * HEADS * HD // P
        HPC = P // HD
        w = sb("p_w", [P, KC, HEADS, 3 * HD], F32)
        wqk = sb("p_wqk", [P, KC, QKM, P], F32)
        wv = sb("p_wv", [P, KC, D], F32)
        ident = sb("p_ident", [P, P], F32)
        x_rows = sb("p_x_rows", [P, CHUNKS, CT, D], F32)
        x_t = sb("p_x_t", [P, CHUNKS, KC, CHUNK], F32)
        parts = sb("p_parts", [P, CHUNKS, QKM, PARTS, CHUNK], BF16)
        rest = sb("p_rest", [P, QKM, CHUNK], F32)
        v_sb = sb("p_v_sb", [P, CHUNKS, CT, HEADS, VW], F32)
        ps_t = pb("p_ps_t", [P, KC, CHUNK], F32)
        ps_qk = pb("p_ps_qk", [P, 2, CHUNK], F32)
        ps_v = pb("p_ps_v", [P, 2, 2, D], F32)

        w_loaded = sem("p_w_loaded")
        w_packed = sem("p_w_packed")
        ident_done = sem("p_ident_done")
        ones_done = sem("p_ones_done")
        x_loaded = [sem(f"p_x_loaded{c}") for c in range(CHUNKS)]
        xt_made = sem("p_xt_made")
        xt_kept = sem("p_xt_kept")
        qk_made = sem("p_qk_made")
        v_made = sem("p_v_made")
        hi_done = sem("p_hi_done")
        rest_done = sem("p_rest_done")
        mid_done = sem("p_mid_done")
        lo_done = sem("p_lo_done")
        v_kept = sem("p_v_kept")
        parts_stored = [sem(f"p_parts_stored{c}") for c in range(CHUNKS)]
        v_stored = [sem(f"p_v_stored{c}") for c in range(CHUNKS)]

        with nc.Block() as block:
            @block.sync
            def _(sp):
                for c in range(KC):
                    sp.dma_start(w[:, c, :, :], w_qkv[:, c * P:(c + 1) * P, :].rearrange("n p e -> p n e"))\
                        .then_inc(w_loaded, 16)

                def load_x(b, c):
                    sp.dma_start(x_rows[:, c, :, :],
                                 x[b].rearrange("(t p) d -> p t d", p=P)[:, c * CT:(c + 1) * CT, :])\
                        .then_inc(x_loaded[c], 16)

                def store(b, c):
                    u = b * CHUNKS + c
                    for m in range(QKM):
                        sp.wait_ge(lo_done, u * QKM + m + 1)
                        sp.dma_start(qk_parts[b, m * P:(m + 1) * P, :, c * CHUNK:(c + 1) * CHUNK],
                                     parts[:, c, m, :, :]).then_inc(parts_stored[c], 16)
                    sp.wait_ge(v_kept, 2 * u + 2)
                    sp.dma_start(v_rows[b].rearrange("t p v -> p t v")[:, c * CT:(c + 1) * CT, :],
                                 v_sb[:, c, :, :, :].rearrange("p t n v -> p t (n v)"))\
                        .then_inc(v_stored[c], 16)

                def turn(b, last):
                    for c in range(CHUNKS):
                        if not last:
                            sp.wait_ge(xt_made, b * CHUNKS + c + 1)
                            load_x(b + 1, c)
                        store(b, c)

                for c in range(CHUNKS):
                    load_x(0, c)
                turn(0, False)
                with sp.Fori(1, BATCH - 1) as b:
                    turn(b, False)
                turn(BATCH - 1, True)
                for c in range(CHUNKS):
                    sp.wait_ge(parts_stored[c], 16 * QKM * BATCH)
                    sp.wait_ge(v_stored[c], 16 * BATCH)

            @block.gpsimd
            def _(pool):
                identity(pool, ident, ident_done)
                def turn(b):
                    for c in range(CHUNKS):
                        u = b * CHUNKS + c
                        pool.wait_ge(parts_stored[c], 16 * QKM * b)
                        for m in range(QKM):
                            pool.wait_ge(mid_done, u * QKM + m + 1)
                            pool.tensor_tensor(parts[:, c, m, 2, :], rest[:, m, :], parts[:, c, m, 1, :],
                                               ALU.subtract).then_inc(lo_done, 1)

                turn(0)
                with pool.Fori(1, BATCH) as b:
                    turn(b)

            @block.vector
            def _(dve):
                dve.memset(v_sb[:, :, :, :, :].rearrange("p c t n v -> p (c t n) v")[:, :, HD:VW], 1.0)\
                   .then_inc(ones_done, 1)
                dve.wait_ge(w_loaded, 16 * KC)
                for qk in range(2):
                    for c in range(KC):
                        dve.tensor_copy(
                            wqk[:, c, qk * QKM // 2:(qk + 1) * QKM // 2, :]
                            .rearrange("p m (n h) -> p (m n) h", h=HD),
                            w[:, c, :, qk * HD:(qk + 1) * HD]).then_inc(w_packed, 1)
                for c in range(KC):
                    dve.tensor_copy(wv[:, c, :].rearrange("p (n h) -> p n h", h=HD),
                                    w[:, c, :, 2 * HD:3 * HD]).then_inc(w_packed, 1)
                def turn(b):
                    for c in range(CHUNKS):
                        u = b * CHUNKS + c
                        dve.wait_ge(lo_done, u * QKM)
                        for m in range(QKM):
                            dve.wait_ge(hi_done, u * QKM + m + 1)
                            dve.tensor_tensor(rest[:, m, :], ps_qk[:, m % 2, :], parts[:, c, m, 0, :],
                                              ALU.subtract).then_inc(rest_done, 1)

                turn(0)
                with dve.Fori(1, BATCH) as b:
                    turn(b)

            @block.scalar
            def _(act):
                act.wait_ge(ones_done, 1)
                def turn(b):
                    for c in range(CHUNKS):
                        u = b * CHUNKS + c
                        act.wait_ge(xt_made, u + 1)
                        act.activation(x_t[:, c, :, :], ps_t[:, :, :], ACT.Copy).then_inc(xt_kept, 1)
                        act.wait_ge(parts_stored[c], 16 * QKM * b)
                        act.wait_ge(v_stored[c], 16 * b)
                        for m in range(QKM):
                            act.wait_ge(qk_made, u * QKM + m + 1)
                            act.activation(parts[:, c, m, 0, :], ps_qk[:, m % 2, :], ACT.Copy)\
                               .then_inc(hi_done, 1)
                            act.wait_ge(rest_done, u * QKM + m + 1)
                            act.activation(parts[:, c, m, 1, :], rest[:, m, :], ACT.Copy)\
                               .then_inc(mid_done, 1)
                        for r in range(2):
                            act.wait_ge(v_made, 2 * u + r + 1)
                            act.activation(v_sb[:, c, 2 * r:2 * r + 2, :, 0:HD],
                                           ps_v[:, r, :, :].rearrange("p t (n h) -> p t n h", h=HD),
                                           ACT.Copy).then_inc(v_kept, 1)

                turn(0)
                with act.Fori(1, BATCH) as b:
                    turn(b)

            @block.tensor
            def _(pe):
                pe.wait_ge(ident_done, 2)
                pe.wait_ge(w_packed, 3 * KC)
                def turn(b):
                    for c in range(CHUNKS):
                        u = b * CHUNKS + c
                        pe.wait_ge(x_loaded[c], 16 * b + 16)
                        pe.wait_ge(xt_kept, u)
                        for k in range(KC):
                            for t in range(CT):
                                last = pe.transpose(ps_t[:, k, t * P:(t + 1) * P],
                                                    x_rows[:, c, t, k * P:(k + 1) * P], ident[:, :])
                        last.then_inc(xt_made, 1)
                        pe.wait_ge(xt_kept, u + 1)
                        for m in range(QKM):
                            pe.wait_ge(rest_done, u * QKM + max(m - 1, 0))
                            for k in range(KC):
                                last = pe.matmul(ps_qk[:, m % 2, :], wqk[:, k, m, :], x_t[:, c, k, :],
                                                 start=(k == 0), stop=(k == KC - 1))
                            last.then_inc(qk_made, 1)
                        pe.wait_ge(v_kept, 2 * u)
                        for r in range(2):
                            for t in range(2):
                                for k in range(KC):
                                    s = (2 * r + t) * P
                                    last = pe.matmul(ps_v[:, r, t, :], x_t[:, c, k, s:s + P], wv[:, k, :],
                                                     start=(k == 0), stop=(k == KC - 1))
                            last.then_inc(v_made, 1)

                turn(0)
                with pe.Fori(1, BATCH) as b:
                    turn(b)


def attend(nc, qk_parts, v_rows, heads_out):
    with ExitStack() as ctx:
        def sb(name, shape, dt):
            return ctx.enter_context(nc.sbuf_tensor(name, shape, dt))

        def pb(name, shape, dt):
            return ctx.enter_context(nc.psum_tensor(name, shape, dt))

        def sem(name):
            return ctx.enter_context(nc.semaphore(name))

        STEPS = [(c, kt) for c in range(CHUNKS) for kt in range(CT * (c + 1))]
        NST = len(STEPS)
        PIECES = [(h, qt, s, min((qt + 1) * P - s, CHUNK), s // CHUNK)
                  for h in range(QUAD) for qt in range(TILES) for s in range(0, (qt + 1) * P, CHUNK)]
        NPC = len(PIECES)
        PPS = NPC // NST
        PB = 3
        LOADS = 16 * (2 * len(TERMS) + 1)

        qs = sb("a_qs", [P, QUADS, QUAD, SEQ], BF16)
        ks = sb("a_ks", [P, QUADS, QUAD, SEQ], BF16)
        vq = sb("a_vq", [P, QUADS, TILES, QUAD, VW], F32)
        probs = sb("a_probs", [P, PB, QUAD, CHUNK], F32)
        ident = sb("a_ident", [P, P], F32)
        ident16 = sb("a_ident16", [P, P], BF16)
        mask16 = sb("a_mask16", [P, P], BF16)
        spread = sb("a_spread", [P, P], F32)
        o_sb = sb("a_o_sb", [P, 2, CHUNK], F32)
        inv = sb("a_inv", [P, 2, CHUNK], F32)
        out_sb = sb("a_out_sb", [P, 2, 64, SEQ // 64], F32)
        mx = sb("a_mx", [P, 2, QUAD, TILES], F32)
        mrow = sb("a_mrow", [QUAD * TILES, PARTS, P], BF16)
        mrest = sb("a_mrest", [QUAD * TILES, P], F32)
        ps_s = pb("a_ps_s", [P, 2, 2, CHUNK], F32)
        ps_m = pb("a_ps_m", [P, 2, CHUNK], F32)
        ps_o = pb("a_ps_o", [P, CHUNK], F32)
        ps_x = pb("a_ps_x", [P, CHUNK], F32)

        ident_done = sem("a_ident_done")
        const_done = sem("a_const_done")
        ones_done = sem("a_ones_done")
        loaded = [sem(f"a_loaded{j}") for j in range(QUADS)]
        rows_made = sem("a_rows_made")
        rows_max = sem("a_rows_max")
        max_done = sem("a_max_done")
        max_t = sem("a_max_t")
        max_split = sem("a_max_split")
        max_sent = sem("a_max_sent")
        scores = sem("a_scores")
        exps = sem("a_exps")
        mask_turn = sem("a_mask_turn")
        masked = sem("a_masked")
        pv_done = sem("a_pv_done")
        o_kept = sem("a_o_kept")
        sums_made = sem("a_sums_made")
        inv_done = sem("a_inv_done")
        out_done = sem("a_out_done")
        out_sent = sem("a_out_sent")

        def step_shape(st):
            c, kt = STEPS[st]
            off = max(kt * P - c * CHUNK, 0)
            return off, CHUNK - off

        with nc.Block() as block:
            @block.sync
            def _(sp):
                def load(b, j):
                    for i, (pq, pk) in enumerate(TERMS):
                        for dst, first, part in ((qs, 0, pq), (ks, HEADS * HD, pk)):
                            r = first + j * QUAD * HD
                            sp.dma_start(dst[i * HD:(i + 1) * HD, j, :, :],
                                         qk_parts[b, r:r + QUAD * HD, part, :]
                                         .rearrange("(n h) s -> h n s", h=HD)).then_inc(loaded[j], 16)
                    sp.dma_start(vq[:, j, :, :, :].rearrange("p t n v -> p t (n v)"),
                                 v_rows[b, :, :, j * QUAD * VW:(j + 1) * QUAD * VW].rearrange("t p v -> p t v"))\
                        .then_inc(loaded[j], 16)

                def send_max(t, j):
                    sp.wait_ge(max_split, 4 * t + 4)
                    for i in range(PARTS):
                        sp.dma_start(qs[TROWS + i:TROWS + i + 1, j, :, :]
                                     .rearrange("o n (t q) -> o (n t) q", q=P),
                                     mrow[:, i, :]).then_inc(max_sent, 16)

                def send_out(b, j):
                    sp.wait_ge(out_done, CHUNKS * (QUADS * b + j + 1))
                    for n in range(QUAD):
                        dst = heads_out[b].rearrange("(r h) (n i) -> n h r i", h=HD, i=SEQ // 64)
                        sp.dma_start(dst[j * QUAD + n], out_sb[n * VW:n * VW + HD, j % 2, :, :])\
                            .then_inc(out_sent, 16)

                for j in range(QUADS):
                    load(0, j)
                for t in range(2):
                    send_max(t, t)

                def turn(b, last):
                    for j in range(QUADS):
                        t = QUADS * b + j
                        if not (last and j + 2 >= QUADS):
                            send_max(t + 2, (j + 2) % QUADS)
                        send_out(b, j)
                        if not last:
                            sp.wait_ge(sums_made, CHUNKS * (t + 1))
                            load(b + 1, j)

                turn(0, False)
                with sp.Fori(1, BATCH - 1) as b:
                    turn(b, False)
                turn(BATCH - 1, True)
                sp.wait_ge(out_sent, 16 * QUAD * SLOTS)

            @block.gpsimd
            def _(pool):
                identity(pool, ident, ident_done)
                pool.memset(mask16[:, :], 0.0).then_inc(const_done, 1)
                pool.memset(spread[:, :], 0.0).then_inc(const_done, 1)
                pool.wait_ge(const_done, 2)
                pool.affine_select(out=mask16[:, :], in_=mask16[:, :], compare_op=ALU.is_ge, fill=NEG,
                                   base=0, pattern=[[-1, P]], channel_multiplier=1).then_inc(const_done, 1)
                by_head = spread[:, :].rearrange("p (n f h) -> p f n h", f=2, h=HD)
                for f in range(2):
                    pool.affine_select(out=by_head[:, f], in_=by_head[:, f], compare_op=ALU.not_equal,
                                       fill=1.0, base=-HD, pattern=[[-VW, QUAD], [-1, HD]],
                                       channel_multiplier=1).then_inc(const_done, 1)
                pool.wait_ge(ident_done, 2)
                pool.tensor_copy(ident16[:, :], ident[:, :]).then_inc(const_done, 1)
                def turn(b):
                    for j in range(QUADS):
                        t = QUADS * b + j
                        n = 0
                        for st, (c, kt) in enumerate(STEPS):
                            if kt < c * CT:
                                continue
                            n += 1
                            pool.wait_ge(exps, 2 * (NST * t + st + 1))
                            pool.sem_inc(mask_turn, 1)
                            tile = probs[:, st % PB, :, 0:P]
                            pool.affine_select(out=tile, in_=tile, compare_op=ALU.is_ge, fill=0.0, base=0,
                                               pattern=[[0, QUAD], [1, P]], channel_multiplier=-1)\
                                .then_inc(masked, 1)

                turn(0)
                with pool.Fori(1, BATCH) as b:
                    turn(b)

            @block.scalar
            def _(act):
                def turn(b):
                    for j in range(QUADS):
                        t = QUADS * b + j

                        def keep_o(c):
                            act.wait_ge(pv_done, NST * t + (CT if c == 0 else NST))
                            act.wait_ge(out_done, CHUNKS * t)
                            act.activation(o_sb[:, c, :], ps_o[:, :], ACT.Copy).then_inc(o_kept, 1)

                        for st, (c, kt) in enumerate(STEPS):
                            off, width = step_shape(st)
                            act.wait_ge(pv_done, NST * t + max(st - PB + 1, 0))
                            for hp in range(2):
                                act.wait_ge(scores, 2 * (NST * t + st) + hp + 1)
                                act.activation(probs[:, st % PB, 2 * hp:2 * hp + 2, 0:width],
                                               ps_s[:, hp, :, 0:width], ACT.Exp, scale=SCALE)\
                                   .then_inc(exps, 1)
                            if st == CT + 1:
                                keep_o(0)
                        keep_o(1)

                turn(0)
                with act.Fori(1, BATCH) as b:
                    turn(b)

            @block.vector
            def _(dve):
                def take_max(v, i):
                    h, qt, s, width, half = PIECES[i]
                    dve.wait_ge(rows_made, NPC * v + i + 1)
                    dve.tensor_reduce(mx[:, half, h, qt:qt + 1], ps_m[:, i % 2, 0:width], AX_X, ALU.max)\
                       .then_inc(rows_max, 1)

                def split_max(v):
                    dve.wait_ge(rows_max, NPC * (v + 1))
                    dve.tensor_tensor(mx[:, 0, :, CT:TILES], mx[:, 0, :, CT:TILES], mx[:, 1, :, CT:TILES],
                                      ALU.max).then_inc(max_done, 1)
                    dve.wait_ge(max_t, v + 1)
                    src = ps_x[0:QUAD * TILES, 0:P]
                    dve.wait_ge(max_sent, 16 * PARTS * v)
                    dve.tensor_scalar(mrow[:, 0, :], src, -1.0, None, ALU.mult).then_inc(max_split, 1)
                    dve.wait_ge(max_split, 4 * v + 1)
                    dve.scalar_tensor_tensor(out=mrest[:, :], in0=src, scalar=-1.0, in1=mrow[:, 0, :],
                                             op0=ALU.mult, op1=ALU.subtract).then_inc(max_split, 1)
                    dve.wait_ge(max_split, 4 * v + 2)
                    dve.tensor_copy(mrow[:, 1, :], mrest[:, :]).then_inc(max_split, 1)
                    dve.wait_ge(max_split, 4 * v + 3)
                    dve.tensor_tensor(mrow[:, 2, :], mrest[:, :], mrow[:, 1, :], ALU.subtract)\
                       .then_inc(max_split, 1)

                def form_out(t, j, c):
                    n = CHUNKS * t + c
                    dve.wait_ge(sums_made, n + 1)
                    dve.reciprocal(inv[:, c, :], ps_x[:, :]).then_inc(inv_done, 1)
                    dve.wait_ge(inv_done, n + 1)
                    dve.wait_ge(out_sent, 16 * QUAD * t)
                    dve.tensor_tensor(out_sb[:, j % 2, :, 8 * c:8 * c + 8].rearrange("p r i -> p i r"),
                                      o_sb[:, c, :].rearrange("p (i r) -> p i r", r=64),
                                      inv[:, c, :].rearrange("p (i r) -> p i r", r=64), ALU.mult)\
                       .then_inc(out_done, 1)

                for j in range(QUADS):
                    dve.memset(ks[TROWS:P, j, :, :], 1.0).then_inc(ones_done, 1)
                for v in range(2):
                    for i in range(NPC):
                        take_max(v, i)
                    split_max(v)

                def turn(b, last):
                    for j in range(QUADS):
                        t = QUADS * b + j
                        more = not (last and j + 2 >= QUADS)
                        for st in range(NST):
                            if more:
                                for i in range(st * PPS, (st + 1) * PPS):
                                    take_max(t + 2, i)
                            if st == CT + 3:
                                form_out(t, j, 0)
                        if more:
                            split_max(t + 2)
                        form_out(t, j, 1)

                turn(0, False)
                with dve.Fori(1, BATCH - 1) as b:
                    turn(b, False)
                turn(BATCH - 1, True)

            @block.tensor
            def _(pe):
                pe.wait_ge(const_done, 6)
                pe.wait_ge(ones_done, QUADS)

                def rows(v, j, i):
                    h, qt, s, width, half = PIECES[i]
                    if i:
                        pe.wait_ge(rows_max, NPC * v + i - 1)
                    else:
                        pe.wait_ge(rows_max, NPC * v)
                    out = ps_m[:, i % 2, :]
                    own = s + width == (qt + 1) * P
                    last = pe.matmul(out[:, 0:width], qs[0:TROWS, j, h, qt * P:(qt + 1) * P],
                                     ks[0:TROWS, j, h, s:s + width], start=True, stop=not own)
                    if own:
                        last = pe.matmul(out[:, width - P:width], ident16[:, :], mask16[:, :],
                                         start=False, stop=True)
                    last.then_inc(rows_made, 1)

                def turn_max(v):
                    pe.wait_ge(max_done, v + 1)
                    pe.transpose(ps_x[0:QUAD * TILES, 0:P], mx[:, 0, :, :].rearrange("p n t -> p (n t)"),
                                 ident[:, :]).then_inc(max_t, 1)

                for v in range(2):
                    pe.wait_ge(loaded[v], LOADS)
                    for i in range(NPC):
                        rows(v, v, i)
                    if v:
                        pe.wait_ge(max_split, 4 * v)
                    turn_max(v)

                def products(t, j, st):
                    c, kt = STEPS[st]
                    off, width = step_shape(st)
                    pe.wait_ge(exps, 2 * (NST * t + st + 1))
                    if kt >= c * CT:
                        own = sum(k >= cc * CT for cc, k in STEPS[:st + 1])
                        pe.wait_ge(masked, TILES * t + own)
                    if kt == 0:
                        pe.wait_ge(o_kept, CHUNKS * t + c)
                    for h in range(QUAD):
                        last = pe.matmul(ps_o[h * VW:(h + 1) * VW, off:CHUNK], vq[:, j, kt, h, :],
                                         probs[:, st % PB, h, 0:width],
                                         start=(kt == 0), stop=(kt == CT * (c + 1) - 1))
                    last.then_inc(pv_done, 1)

                def sums(t, c):
                    pe.wait_ge(o_kept, CHUNKS * t + c + 1)
                    pe.matmul(ps_x[:, :], spread[:, :], o_sb[:, c, :], start=True, stop=True)\
                      .then_inc(sums_made, 1)

                def turn(b, last):
                    for j in range(QUADS):
                        t = QUADS * b + j
                        more = not (last and j + 2 >= QUADS)
                        jm = (j + 2) % QUADS
                        pe.wait_ge(max_sent, 16 * PARTS * (t + 1))
                        if more:
                            pe.wait_ge(loaded[jm], LOADS * (b + 1 + (j + 2) // QUADS))
                        for st, (c, kt) in enumerate(STEPS):
                            off, width = step_shape(st)
                            q0 = c * CHUNK + off
                            for hp in range(2):
                                pe.wait_ge(exps, 2 * (NST * t + st) + hp - 1 if st else 2 * NST * t)
                                for h in range(2):
                                    n = 2 * hp + h
                                    s = pe.matmul(ps_s[:, hp, h, 0:width],
                                                  ks[0:MROWS, j, n, kt * P:(kt + 1) * P],
                                                  qs[0:MROWS, j, n, q0:q0 + width], start=True, stop=True)
                                s.then_inc(scores, 1)
                            if more:
                                for i in range(st * PPS, (st + 1) * PPS):
                                    rows(t + 2, jm, i)
                            if st >= 1:
                                products(t, j, st - 1)
                            if st == CT + 3:
                                pe.wait_ge(inv_done, CHUNKS * t)
                                if not (last and j == QUADS - 1):
                                    pe.wait_ge(max_split, 4 * (t + 2))
                                sums(t, 0)
                        if more:
                            pe.wait_ge(inv_done, CHUNKS * t + 1)
                            turn_max(t + 2)
                        products(t, j, NST - 1)
                        pe.wait_ge(inv_done, CHUNKS * t + 1)
                        if more:
                            pe.wait_ge(max_split, 4 * (t + 3))
                        sums(t, 1)

                turn(0, False)
                with pe.Fori(1, BATCH - 1) as b:
                    turn(b, False)
                turn(BATCH - 1, True)


def feed(nc, x, heads_out, w_out, mix_kernel, w1, b1, w2, b2, wo1, bo1, wo2, bo2, gamma, beta, out):
    with ExitStack() as ctx:
        def sb(name, shape, dt):
            return ctx.enter_context(nc.sbuf_tensor(name, shape, dt))

        def pb(name, shape, dt):
            return ctx.enter_context(nc.psum_tensor(name, shape, dt))

        def sem(name):
            return ctx.enter_context(nc.semaphore(name))

        PATHS, _, DM = w1.shape
        MC = (PATHS + 1) * DM // P
        LAST = MC - 1
        EPS = 1e-5
        X2 = DM + PATHS

        w1_sb = sb("f_w1", [P, KC, PATHS + 1, DM], F32)
        w2_sb = sb("f_w2", [P, MC, D], F32)
        wo2_sb = sb("f_wo2", [P, PATHS], F32)
        bias = sb("f_bias", [P, MC], F32)
        mixk = sb("f_mixk", [P, 3, KC], F32)
        wout_sb = sb("f_wout", [P, HEADS * HD // P, D], F32)
        row = sb("f_row", [1, 2 * D + PATHS], F32)
        ones = sb("f_ones", [P, P], F32)
        wsum = sb("f_wsum", [P, D], F32)
        gb = sb("f_gb", [P, 2, D], F32)
        bo2_sb = sb("f_bo2", [P, PATHS], F32)
        prio = sb("f_prio", [P, PATHS], F32)
        ident = sb("f_ident", [P, P], F32)
        ident16 = sb("f_ident16", [P, P], BF16)
        widen = sb("f_widen", [P, PATHS + 1, DM], BF16)
        half = sb("f_half", [P, TILES], F32)

        x_in = sb("f_x_in", [P, TILES, D], F32)
        a_in = sb("f_a_in", [P, TILES, D], F32)
        aw = sb("f_aw", [P, TILES, D], F32)
        x1 = sb("f_x1", [P, 2, TILES, D], F32)
        x1_t = sb("f_x1_t", [P, KC, SEQ + 2], F32)
        xm = sb("f_xm", [P, 2, KC, SEQ], F32)
        mixa = sb("f_mixa", [P, 2, SEQ], F32)
        st_a = sb("f_st_a", [P, TILES, 6], F32)
        mv_a = sb("f_mv_a", [P, TILES, 2], F32)
        ve_a = sb("f_ve_a", [P, TILES], F32)
        rs_a = sb("f_rs_a", [P, TILES], F32)

        hid = sb("f_hid", [P, MC, CHUNK], F32)
        hm = sb("f_hm", [P, MC, CHUNK], F32)
        sc = sb("f_sc", [P, CT, PATHS], F32)
        eq = sb("f_eq", [P, CT, PATHS], F32)
        best = sb("f_best", [P, 2, CT], F32)
        pick = sb("f_pick", [P, CT, PATHS], BF16)
        pick_t = sb("f_pick_t", [P, CHUNK], BF16)
        y = sb("f_y", [P, CT, D], F32)
        z = sb("f_z", [P, CT, D], F32)
        xb = sb("f_xb", [P, CT, D], F32)
        st_b = sb("f_st_b", [P, CT, 6], F32)
        mv_b = sb("f_mv_b", [P, CT, 2], F32)
        ve_b = sb("f_ve_b", [P, CT], F32)
        rs_b = sb("f_rs_b", [P, 2, CT], F32)
        res = sb("f_res", [P, 2, CT, D], F32)

        ps_t = pb("f_ps_t", [P, 2, CHUNK], F32)
        ps_h = pb("f_ps_h", [P, 2, CHUNK], F32)
        ps_k = pb("f_ps_k", [P, CHUNK], F32)
        ps_o = pb("f_ps_o", [P, 2, 2, D], F32)
        ps_c = pb("f_ps_c", [P, CHUNK], F32)
        ps_pick = ps_c[:, CHUNK // 2:CHUNK].bitcast(BF16)

        w_loaded = sem("f_w_loaded")
        const_done = sem("f_const_done")
        pool_const = sem("f_pool_const")
        bcast_made = sem("f_bcast_made")
        bcast_kept = sem("f_bcast_kept")
        in_loaded = sem("f_in_loaded")
        in_used = sem("f_in_used")
        aw_done = sem("f_aw_done")
        ve_done = sem("f_ve_done")
        rs_done = sem("f_rs_done")
        x1_done = sem("f_x1_done")
        xt_made = sem("f_xt_made")
        xt_kept = sem("f_xt_kept")
        xm_done = sem("f_xm_done")
        chain = sem("f_chain")
        h_made = sem("f_h_made")
        h_kept = sem("f_h_kept")
        sc_made = sem("f_sc_made")
        picked = sem("f_picked")
        pick_made = sem("f_pick_made")
        pick_kept = sem("f_pick_kept")
        k_made = sem("f_k_made")
        hm_done = sem("f_hm_done")
        o_made = sem("f_o_made")
        y_done = sem("f_y_done")
        xb_done = sem("f_xb_done")
        carrier = sem("f_carrier")
        res_done = sem("f_res_done")
        stored = sem("f_stored")

        def turns(eng, turn):
            for e in range(2):
                turn(e, e, False)
            with eng.Fori(1, BATCH // 2 - 1) as pair:
                for e in range(2):
                    turn(2 * pair + e, e, False)
            for e in range(2):
                turn(BATCH - 2 + e, e, e == 1)

        with nc.Block() as block:
            @block.sync
            def _(sp):
                def load_in(b):
                    sp.dma_start(x_in[:, :, :], x[b].rearrange("(t p) d -> p t d", p=P)).then_inc(in_loaded, 16)
                    sp.dma_start(a_in[:, :, :], heads_out[b].rearrange("(t p) d -> p t d", p=P))\
                        .then_inc(in_loaded, 16)

                load_in(0)
                sp.dma_start(wout_sb[:, :, :], w_out.rearrange("(a n) h d -> (n h) a d", n=P // HD))\
                    .then_inc(w_loaded, 16)
                for i, v in enumerate((gamma, beta)):
                    sp.dma_start(row[:, i * D:(i + 1) * D], v.rearrange("(a d) -> a d", a=1)).then_inc(w_loaded, 16)
                sp.dma_start(row[:, 2 * D:2 * D + PATHS], bo2.rearrange("(a d) -> a d", a=1)).then_inc(w_loaded, 16)
                for k in range(KC):
                    rows = slice(k * P, (k + 1) * P)
                    sp.dma_start(w1_sb[:, k, 0:PATHS, :], w1[:, rows, :].rearrange("p d m -> d p m"))\
                        .then_inc(w_loaded, 16)
                    sp.dma_start(w1_sb[:, k, PATHS, :], wo1[rows, :]).then_inc(w_loaded, 16)
                    sp.dma_start(mixk[:, :, k], mix_kernel[:, rows].rearrange("t d -> d t"),
                                 allow_slow_non_contiguous=True).then_inc(w_loaded, 16)
                for m in range(LAST):
                    sp.dma_start(w2_sb[:, m, :], w2[2 * m:2 * m + 2].rearrange("q m d -> (q m) d"))\
                        .then_inc(w_loaded, 16)
                    sp.dma_start(bias[:, m:m + 1],
                                 b1[2 * m:2 * m + 2].rearrange("q (m o) -> (q m) o", o=1)).then_inc(w_loaded, 16)
                sp.dma_start(w2_sb[0:DM, LAST, :], w2[PATHS - 1]).then_inc(w_loaded, 16)
                sp.dma_start(w2_sb[DM:X2, LAST, :], b2).then_inc(w_loaded, 16)
                sp.dma_start(bias[0:DM, LAST:MC], b1[PATHS - 1].rearrange("(m o) -> m o", o=1)).then_inc(w_loaded, 16)
                sp.dma_start(bias[DM:P, LAST:MC], bo1.rearrange("(m o) -> m o", o=1)).then_inc(w_loaded, 16)
                sp.dma_start(wo2_sb[DM:P, :], wo2).then_inc(w_loaded, 16)

                def turn(b, e, last):
                    if not last:
                        sp.wait_ge(in_used, b + 1)
                        load_in_next(b + 1)
                    for c in range(CHUNKS):
                        n = CHUNKS * b + c
                        sp.wait_ge(res_done, n + 1)
                        sp.dma_start(out[b].rearrange("(t p) d -> p t d", p=P)[:, c * CT:(c + 1) * CT, :],
                                     res[:, c, :, :]).then_inc(stored, 16)

                load_in_next = load_in
                turns(sp, turn)
                sp.wait_ge(stored, 16 * CHUNKS * BATCH)

            WL = 16 * (4 + 3 * KC + 2 * LAST + 5)

            @block.gpsimd
            def _(pool):
                identity(pool, ident, const_done)
                pool.memset(ones[:, :], 1.0).then_inc(pool_const, 1)
                pool.memset(widen[:, :, :], 0.0).then_inc(pool_const, 1)
                pool.memset(half[:, :], -0.5).then_inc(pool_const, 1)
                pool.memset(pick_t[:, :], 0.0).then_inc(pool_const, 1)
                for k in range(KC):
                    pool.memset(x1_t[:, k, 0:SEQ + 2:SEQ + 1], 0.0).then_inc(pool_const, 1)
                for p in range(PATHS):
                    pool.memset(prio[:, p:p + 1], float(PATHS - p)).then_inc(pool_const, 1)
                pool.wait_ge(const_done, 2)
                pool.tensor_copy(ident16[:, :], ident[:, :]).then_inc(pool_const, 1)
                pool.wait_ge(pool_const, 5 + KC + PATHS)
                pool.affine_select(out=widen[:, :, :], in_=widen[:, :, :], compare_op=ALU.not_equal, fill=1.0,
                                   base=0, pattern=[[-1, PATHS + 1], [0, DM]], channel_multiplier=1)\
                    .then_inc(pool_const, 1)
                pool.wait_ge(bcast_kept, 4)

                def rsqrt(count, ve, rs, k):
                    pool.wait_ge(ve_done, count)
                    pool.tensor_tensor(rs, ve, half[:, 0:k], ALU.pow).then_inc(rs_done, 1)

                def stage_a(b, before):
                    pool.wait_ge(x1_done, b)
                    pool.wait_ge(in_loaded, 32 * (b + 1))
                    pool.tensor_tensor(aw[:, :, :], a_in[:, :, :],
                                       wsum[:, :].rearrange("p (o d) -> p o d", o=1).broadcast_to((P, TILES, D)),
                                       ALU.mult).then_inc(aw_done, 1)
                    rsqrt(before + 1, ve_a[:, :], rs_a[:, :], TILES)

                def turn(b, e, last):
                    for c in range(CHUNKS):
                        n = CHUNKS * b + c
                        if c == 0 and not last:
                            stage_a(b + 1, 1 + 5 * b)
                        base = 5 * b + (2 if not last else 1) + 2 * c
                        pool.wait_ge(res_done, n)
                        pool.wait_ge(x1_done, b + 1)
                        pool.tensor_tensor(xb[:, :, :], x1[:, e, c * CT:(c + 1) * CT, :],
                                           gb[:, 1, :].rearrange("p (o d) -> p o d", o=1).broadcast_to((P, CT, D)),
                                           ALU.add).then_inc(xb_done, 1)
                        for i in range(2):
                            rsqrt(base + i + 1, ve_b[:, :], rs_b[:, i, :], CT)

                stage_a(0, 0)
                turns(pool, turn)

            @block.scalar
            def _(act):
                act.wait_ge(bcast_made, 1)
                act.activation(wsum[:, :], ps_o[:, 0, 0, :], ACT.Copy).then_inc(bcast_kept, 1)
                for i in range(2):
                    act.wait_ge(bcast_made, i + 2)
                    act.activation(gb[:, i, :], ps_h[:, i, 0:D], ACT.Copy).then_inc(bcast_kept, 1)
                act.wait_ge(bcast_made, 4)
                act.activation(bo2_sb[:, :], ps_c[:, 0:PATHS], ACT.Copy).then_inc(bcast_kept, 1)
                act.wait_ge(w_loaded, WL)

                def stage_a(b):
                    act.wait_ge(xm_done, b)
                    for g in range(CHUNKS):
                        for k in range(KC):
                            act.wait_ge(xt_made, 4 * b + 2 * g + k + 1)
                            act.activation(x1_t[:, k, 1 + g * CHUNK:1 + (g + 1) * CHUNK], ps_t[:, k, :],
                                           ACT.Copy).then_inc(xt_kept, 1)

                def turn(b, e, last):
                    for c in range(CHUNKS):
                        n = CHUNKS * b + c
                        act.wait_ge(hm_done, MC * n)
                        act.wait_ge(h_made, MC * n + 1)
                        act.activation(hid[DM:P, LAST, :], ps_h[DM:P, 0, :], ACT.Tanh,
                                       bias=bias[DM:P, LAST:MC]).then_inc(h_kept, 1)
                        act.activation(hid[0:DM, LAST, :], ps_h[0:DM, 0, :], ACT.Identity,
                                       bias=bias[0:DM, LAST:MC]).then_inc(h_kept, 1)
                        for m in range(LAST):
                            act.wait_ge(h_made, MC * n + m + 2)
                            act.activation(hid[:, m, :], ps_h[:, (m + 1) % 2, :], ACT.Identity,
                                           bias=bias[:, m:m + 1]).then_inc(h_kept, 1)
                        act.wait_ge(pick_made, n + 1)
                        act.activation(pick_t[0:PATHS, :], ps_pick[0:PATHS, :], ACT.Copy).then_inc(pick_kept, 1)
                        act.wait_ge(o_made, 2 * n)
                        act.activation(hm[DM:X2, LAST, :], ps_pick[0:PATHS, :], ACT.Copy).then_inc(pick_kept, 1)
                        if c == 0 and not last:
                            stage_a(b + 1)

                stage_a(0)
                turns(act, turn)

            @block.vector
            def _(dve):
                dve.wait_ge(bcast_kept, 4)
                dve.wait_ge(w_loaded, WL)
                links = [0]

                def link(ins, turn):
                    base, total = turn
                    links[0] += 1
                    ins.then_inc(chain, 1)
                    dve.wait_ge(chain, base + links[0])

                def statistics(src, tiles, st, mv, ve, at):
                    for i in range(tiles):
                        ins = dve.bn_stats(st[:, i, :], src[:, i, :])
                    link(ins, at)
                    dve.sem_inc(carrier, 1)
                    for i in range(tiles):
                        ins = dve.bn_aggr(mv[:, i, :], st[:, i, :])
                    link(ins, at)
                    dve.tensor_scalar(ve, mv[:, :, 1], EPS, None, ALU.add).then_inc(ve_done, 1)

                def layernorm(b, e, at):
                    dve.wait_ge(in_loaded, 32 * (b + 1))
                    dve.wait_ge(aw_done, b + 1)
                    ins = dve.tensor_tensor(aw[:, :, :], aw[:, :, :], x_in[:, :, :], ALU.add)
                    ins.then_inc(in_used, 1)
                    dve.wait_ge(in_used, b + 1)
                    dve.sem_inc(carrier, 1)
                    statistics(aw, TILES, st_a, mv_a, ve_a[:, :], at)

                def normalize(b, e, count):
                    dve.wait_ge(rs_done, count)
                    for i in range(TILES):
                        ins = dve.tensor_scalar(x1[:, e, i, :], aw[:, i, :], mv_a[:, i, 0:1], rs_a[:, i:i + 1],
                                                ALU.subtract, ALU.mult)
                    ins.then_inc(x1_done, 1)

                def mix(b, e, at):
                    dve.wait_ge(xt_kept, 4 * (b + 1))
                    for k in range(KC):
                        link(dve.tensor_scalar(mixa[:, 0, :], x1_t[:, k, 0:SEQ], mixk[:, 0, k:k + 1], None,
                                               ALU.mult), at)
                        link(dve.scalar_tensor_tensor(out=mixa[:, 1, :], in0=x1_t[:, k, 1:SEQ + 1],
                                                      scalar=mixk[:, 1, k:k + 1], in1=mixa[:, 0, :],
                                                      op0=ALU.mult, op1=ALU.add), at)
                        ins = dve.scalar_tensor_tensor(out=xm[:, e, k, :], in0=x1_t[:, k, 2:SEQ + 2],
                                                       scalar=mixk[:, 2, k:k + 1], in1=mixa[:, 1, :],
                                                       op0=ALU.mult, op1=ALU.add)
                        if k < KC - 1:
                            link(ins, at)
                    ins.then_inc(xm_done, 1)

                def choose(n, at):
                    dve.wait_ge(sc_made, n + 1)
                    link(dve.tensor_tensor(sc[:, :, :],
                                           ps_c[:, 0:CT * PATHS].rearrange("p (t q) -> p t q", q=PATHS),
                                           bo2_sb[:, :].rearrange("p (o q) -> p o q", o=1).broadcast_to((P, CT, PATHS)),
                                           ALU.add), at)
                    link(dve.tensor_reduce(best[:, 0, :], sc[:, :, :], AX_X, ALU.max), at)
                    link(dve.tensor_tensor(eq[:, :, :], sc[:, :, :],
                                           best[:, 0, :].rearrange("p (t o) -> p t o", o=1).broadcast_to((P, CT, PATHS)),
                                           ALU.is_equal), at)
                    link(dve.tensor_tensor(sc[:, :, :], eq[:, :, :],
                                           prio[:, :].rearrange("p (o q) -> p o q", o=1).broadcast_to((P, CT, PATHS)),
                                           ALU.mult), at)
                    link(dve.tensor_reduce(best[:, 1, :], sc[:, :, :], AX_X, ALU.max), at)
                    dve.tensor_tensor(pick[:, :, :], sc[:, :, :],
                                      best[:, 1, :].rearrange("p (t o) -> p t o", o=1).broadcast_to((P, CT, PATHS)),
                                      ALU.is_equal).then_inc(picked, 1)

                def turn(b, e, last):
                    total = TOTAL if not last else None
                    at = (A0 + TOTAL * b, total)
                    links[0] = 0
                    for c in range(CHUNKS):
                        n = CHUNKS * b + c
                        choose(n, at)
                        dve.wait_ge(o_made, 2 * n)
                        for i, m in enumerate(list(range(LAST)) + [LAST]):
                            rows = P if m < LAST else DM
                            dve.wait_ge(k_made, MC * n + i + 1)
                            dve.wait_ge(h_kept, (MC + 1) * (n + 1))
                            dve.tensor_tensor(hm[0:rows, m, :], ps_k[0:rows, :], hid[0:rows, m, :], ALU.mult)\
                               .then_inc(hm_done, 1)
                        if not last:
                            if c == 0:
                                layernorm(b + 1, 1 - e, at)
                                normalize(b + 1, 1 - e, 5 * b + 2)
                            else:
                                mix(b + 1, 1 - e, at)
                        base = 5 * b + (2 if not last else 1) + 2 * c
                        tiles = slice(c * CT, (c + 1) * CT)
                        for r in range(2):
                            dve.wait_ge(o_made, 2 * n + r + 1)
                            dve.tensor_tensor(y[:, 2 * r:2 * r + 2, :], ps_o[:, r, :, :],
                                              x1[:, e, c * CT + 2 * r:c * CT + 2 * r + 2, :], ALU.add)\
                               .then_inc(y_done, 1)
                        dve.wait_ge(y_done, 2 * n + 2)
                        dve.sem_inc(carrier, 1)
                        statistics(y, CT, st_b, mv_b, ve_b[:, :], at)
                        dve.wait_ge(rs_done, base + 1)
                        for i in range(CT):
                            ins = dve.tensor_scalar(z[:, i, :], y[:, i, :], mv_b[:, i, 0:1], rs_b[:, 0, i:i + 1],
                                                    ALU.subtract, ALU.mult)
                        link(ins, at)
                        link(dve.tensor_tensor(y[:, :, :], z[:, :, :],
                                               gb[:, 0, :].rearrange("p (o d) -> p o d", o=1).broadcast_to((P, CT, D)),
                                               ALU.mult), at)
                        dve.wait_ge(xb_done, n + 1)
                        link(dve.tensor_tensor(z[:, :, :], y[:, :, :], xb[:, :, :], ALU.add), at)
                        dve.sem_inc(carrier, 1)
                        statistics(z, CT, st_b, mv_b, ve_b[:, :], at)
                        dve.wait_ge(stored, 16 * CHUNKS * b)
                        dve.wait_ge(rs_done, base + 2)
                        for i in range(CT):
                            ins = dve.tensor_scalar(res[:, c, i, :], z[:, i, :], mv_b[:, i, 0:1],
                                                    rs_b[:, 1, i:i + 1], ALU.subtract, ALU.mult)
                        ins.then_inc(res_done, 1)
                    assert last or links[0] == TOTAL, links

                A0, TOTAL = 2 + 5, 2 * 5 + 2 + 5 + 2 * (2 + 3 + 2)
                layernorm(0, 0, (0, None))
                normalize(0, 0, 1)
                mix(0, 0, (0, None))
                assert links[0] == A0, links
                turns(dve, turn)

            @block.tensor
            def _(pe):
                pe.wait_ge(w_loaded, WL)
                pe.wait_ge(pool_const, 6 + KC + PATHS)
                WC = HEADS * HD // P
                for a in range(WC):
                    last_mm = pe.matmul(ps_o[:, 0, 0, :], ones[:, :], wout_sb[:, a, :],
                                        start=(a == 0), stop=(a == WC - 1))
                last_mm.then_inc(bcast_made, 1)
                for i in range(2):
                    pe.matmul(ps_h[:, i, 0:D], ones[0:1, :], row[:, i * D:(i + 1) * D], start=True, stop=True)\
                      .then_inc(bcast_made, 1)
                pe.matmul(ps_c[:, 0:PATHS], ones[0:1, :], row[:, 2 * D:2 * D + PATHS], start=True, stop=True)\
                  .then_inc(bcast_made, 1)
                pe.wait_ge(bcast_kept, 4)

                def stage_a(b, e):
                    pe.wait_ge(x1_done, b + 1)
                    for g in range(CHUNKS):
                        for k in range(KC):
                            pe.wait_ge(xt_kept, 4 * b + 2 * g if g else 4 * b)
                            for t in range(CT):
                                ins = pe.transpose(ps_t[:, k, t * P:(t + 1) * P],
                                                   x1[:, e, g * CT + t, k * P:(k + 1) * P], ident[:, :])
                            ins.then_inc(xt_made, 1)

                def turn(b, e, last):
                    pe.wait_ge(xm_done, b + 1)
                    for c in range(CHUNKS):
                        n = CHUNKS * b + c

                        def hidden(i):
                            m = LAST if i == 0 else i - 1
                            if i >= 1:
                                pe.wait_ge(h_kept, (MC + 1) * n + (0 if i == 1 else i))
                            else:
                                pe.wait_ge(h_kept, (MC + 1) * n)
                            for k in range(KC):
                                ins = pe.matmul(ps_h[:, i % 2, :],
                                                w1_sb[:, k, 2 * m:2 * m + 2, :].rearrange("d p m -> d (p m)"),
                                                xm[:, e, k, c * CHUNK:(c + 1) * CHUNK],
                                                start=(k == 0), stop=(k == KC - 1))
                            ins.then_inc(h_made, 1)

                        hidden(0)
                        hidden(1)
                        pe.wait_ge(h_kept, (MC + 1) * n + 1)
                        for t in range(CT):
                            ins = pe.matmul(ps_c[:, t * PATHS:(t + 1) * PATHS], hid[DM:P, LAST, t * P:(t + 1) * P],
                                            wo2_sb[DM:P, :], start=True, stop=True)
                        ins.then_inc(sc_made, 1)
                        for i in range(2, MC):
                            hidden(i)
                        pe.wait_ge(picked, n + 1)
                        for t in range(CT):
                            ins = pe.transpose(ps_pick[0:PATHS, t * P:(t + 1) * P], pick[:, t, :], ident16[:, :])
                        ins.then_inc(pick_made, 1)
                        pe.wait_ge(pick_kept, 2 * n + 1)
                        for i in range(MC):
                            pe.wait_ge(hm_done, MC * n + i)
                            pe.matmul(ps_k[:, :], widen[:, 2 * i:2 * i + 2, :].rearrange("p q m -> p (q m)"),
                                      pick_t[:, :], start=True, stop=True).then_inc(k_made, 1)
                        pe.wait_ge(hm_done, MC * (n + 1))
                        pe.wait_ge(pick_kept, 2 * n + 2)
                        for t in range(CT):
                            if t % 2 == 0:
                                pe.wait_ge(y_done, 2 * n)
                            for m in range(MC):
                                rows = P if m < LAST else X2
                                ins = pe.matmul(ps_o[:, t // 2, t % 2, :], hm[0:rows, m, t * P:(t + 1) * P],
                                                w2_sb[0:rows, m, :], start=(m == 0), stop=(m == LAST))
                            if t % 2:
                                ins.then_inc(o_made, 1)
                        if c == 0 and not last:
                            stage_a(b + 1, 1 - e)

                stage_a(0, 0)
                turns(pe, turn)


_INS = ['L0_attn_x', 'L0_attn_W_qkv', 'L0_attn_W_out', 'L0_ffn_mix_kernel', 'L0_ffn_W1', 'L0_ffn_b1',
        'L0_ffn_W2', 'L0_ffn_b2', 'L0_ffn_Wo1', 'L0_ffn_bo1', 'L0_ffn_Wo2', 'L0_ffn_bo2',
        'L0_ffn_gamma', 'L0_ffn_beta']


def layer(nc, x, w_qkv, w_out, mix_kernel, w1, b1, w2, b2, wo1, bo1, wo2, bo2, gamma, beta, out):
    qk_parts = nc.dram_tensor("qk_parts", (BATCH, 2 * HEADS * HD, PARTS, SEQ), BF16).ap()
    v_rows = nc.dram_tensor("v_rows", (BATCH, TILES, P, HEADS * VW), F32).ap()
    heads_out = nc.dram_tensor("heads_out", (BATCH, SEQ, D), F32).ap()
    project(nc, x, w_qkv, qk_parts, v_rows)
    attend(nc, qk_parts, v_rows, heads_out)
    feed(nc, x, heads_out, w_out, mix_kernel, w1, b1, w2, b2, wo1, bo1, wo2, bo2, gamma, beta, out)


def kernel(**inputs):
    import numpy as _np
    import concourse.bacc as _bacc
    from concourse import mybir as _mybir
    from concourse.bass_utils import run_bass_kernel_spmd as _run

    nc = _bacc.Bacc("TRN2", target_bir_lowering=False, num_devices=1)
    arrays, args = {}, []
    for name in _INS:
        a = _np.ascontiguousarray(inputs[name])
        arrays[f"in_{name}_dram"] = a
        args.append(nc.dram_tensor(f"in_{name}_dram", a.shape, _mybir.dt.from_np(a.dtype), kind="ExternalInput").ap())
    out = nc.dram_tensor("out_0_dram", (BATCH, SEQ, D), F32, kind="ExternalOutput").ap()
    layer(nc, *args, out)
    r = _run(nc, [arrays], core_ids=[0])
    return r.results[0]["out_0_dram"]
```

```python
from contextlib import ExitStack

import concourse.bass as bass
from concourse import mybir

ALU = mybir.AluOpType
ACT = mybir.ActivationFunctionType
AX_X = mybir.AxisListType.X
F32 = mybir.dt.float32
BF16 = mybir.dt.bfloat16

P = 128
BATCH, SEQ, D = 8, 1024, 256
HEADS, HD = 16, 16
KC = D // P
TILES = SEQ // P
CHUNK = 512
CHUNKS = SEQ // CHUNK
CT = CHUNK // P
QUAD = 4
QUADS = HEADS // QUAD
SLOTS = BATCH * QUADS
PARTS = 3
TERMS = [(0, 0), (0, 1), (0, 2), (1, 0), (1, 1), (2, 0)]
TROWS = len(TERMS) * HD
MROWS = TROWS + PARTS
SCALE = 0.25
NEG = -4.0e10
VW = 2 * HD


def identity(eng, tile, done):
    eng.memset(tile[:, :], 0.0).then_inc(done, 1)
    eng.wait_ge(done, 1)
    eng.affine_select(out=tile[:, :], in_=tile[:, :], compare_op=ALU.not_equal, fill=1.0,
                      base=0, pattern=[[-1, P]], channel_multiplier=1).then_inc(done, 1)


def project(nc, x, w_qkv, qk_parts, v_rows):
    with ExitStack() as ctx:
        def sb(name, shape, dt):
            return ctx.enter_context(nc.sbuf_tensor(name, shape, dt))

        def pb(name, shape, dt):
            return ctx.enter_context(nc.psum_tensor(name, shape, dt))

        def sem(name):
            return ctx.enter_context(nc.semaphore(name))

        QKM = 2 * HEADS * HD // P
        HPC = P // HD
        w = sb("p_w", [P, KC, HEADS, 3 * HD], F32)
        wqk = sb("p_wqk", [P, KC, QKM, P], F32)
        wv = sb("p_wv", [P, KC, D], F32)
        ident = sb("p_ident", [P, P], F32)
        x_rows = sb("p_x_rows", [P, CHUNKS, CT, D], F32)
        x_t = sb("p_x_t", [P, CHUNKS, KC, CHUNK], F32)
        parts = sb("p_parts", [P, CHUNKS, QKM, PARTS, CHUNK], BF16)
        rest = sb("p_rest", [P, QKM, CHUNK], F32)
        v_sb = sb("p_v_sb", [P, CHUNKS, CT, HEADS, VW], F32)
        ps_t = pb("p_ps_t", [P, KC, CHUNK], F32)
        ps_qk = pb("p_ps_qk", [P, 2, CHUNK], F32)
        ps_v = pb("p_ps_v", [P, 2, 2, D], F32)

        w_loaded = sem("p_w_loaded")
        w_packed = sem("p_w_packed")
        ident_done = sem("p_ident_done")
        ones_done = sem("p_ones_done")
        x_loaded = [sem(f"p_x_loaded{c}") for c in range(CHUNKS)]
        xt_made = sem("p_xt_made")
        xt_kept = sem("p_xt_kept")
        qk_made = sem("p_qk_made")
        v_made = sem("p_v_made")
        hi_done = sem("p_hi_done")
        rest_done = sem("p_rest_done")
        mid_done = sem("p_mid_done")
        lo_done = sem("p_lo_done")
        v_kept = sem("p_v_kept")
        parts_stored = [sem(f"p_parts_stored{c}") for c in range(CHUNKS)]
        v_stored = [sem(f"p_v_stored{c}") for c in range(CHUNKS)]

        with nc.Block() as block:
            @block.sync
            def _(sp):
                for c in range(KC):
                    sp.dma_start(w[:, c, :, :], w_qkv[:, c * P:(c + 1) * P, :].rearrange("n p e -> p n e"))\
                        .then_inc(w_loaded, 16)

                def load_x(b, c):
                    sp.dma_start(x_rows[:, c, :, :],
                                 x[b].rearrange("(t p) d -> p t d", p=P)[:, c * CT:(c + 1) * CT, :])\
                        .then_inc(x_loaded[c], 16)

                def store(b, c):
                    u = b * CHUNKS + c
                    for m in range(QKM):
                        sp.wait_ge(lo_done, u * QKM + m + 1)
                        sp.dma_start(qk_parts[b, m * P:(m + 1) * P, :, c * CHUNK:(c + 1) * CHUNK],
                                     parts[:, c, m, :, :]).then_inc(parts_stored[c], 16)
                    sp.wait_ge(v_kept, 2 * u + 2)
                    sp.dma_start(v_rows[b].rearrange("t p v -> p t v")[:, c * CT:(c + 1) * CT, :],
                                 v_sb[:, c, :, :, :].rearrange("p t n v -> p t (n v)"))\
                        .then_inc(v_stored[c], 16)

                def turn(b, last):
                    for c in range(CHUNKS):
                        if not last:
                            sp.wait_ge(xt_made, b * CHUNKS + c + 1)
                            load_x(b + 1, c)
                        store(b, c)

                for c in range(CHUNKS):
                    load_x(0, c)
                turn(0, False)
                with sp.Fori(1, BATCH - 1) as b:
                    turn(b, False)
                turn(BATCH - 1, True)
                for c in range(CHUNKS):
                    sp.wait_ge(parts_stored[c], 16 * QKM * BATCH)
                    sp.wait_ge(v_stored[c], 16 * BATCH)

            @block.gpsimd
            def _(pool):
                identity(pool, ident, ident_done)
                def turn(b):
                    for c in range(CHUNKS):
                        u = b * CHUNKS + c
                        pool.wait_ge(parts_stored[c], 16 * QKM * b)
                        for m in range(QKM):
                            pool.wait_ge(mid_done, u * QKM + m + 1)
                            pool.tensor_tensor(parts[:, c, m, 2, :], rest[:, m, :], parts[:, c, m, 1, :],
                                               ALU.subtract).then_inc(lo_done, 1)

                turn(0)
                with pool.Fori(1, BATCH) as b:
                    turn(b)

            @block.vector
            def _(dve):
                dve.memset(v_sb[:, :, :, :, :].rearrange("p c t n v -> p (c t n) v")[:, :, HD:VW], 1.0)\
                   .then_inc(ones_done, 1)
                dve.wait_ge(w_loaded, 16 * KC)
                for qk in range(2):
                    for c in range(KC):
                        dve.tensor_copy(
                            wqk[:, c, qk * QKM // 2:(qk + 1) * QKM // 2, :]
                            .rearrange("p m (n h) -> p (m n) h", h=HD),
                            w[:, c, :, qk * HD:(qk + 1) * HD]).then_inc(w_packed, 1)
                for c in range(KC):
                    dve.tensor_copy(wv[:, c, :].rearrange("p (n h) -> p n h", h=HD),
                                    w[:, c, :, 2 * HD:3 * HD]).then_inc(w_packed, 1)
                def turn(b):
                    for c in range(CHUNKS):
                        u = b * CHUNKS + c
                        dve.wait_ge(lo_done, u * QKM)
                        for m in range(QKM):
                            dve.wait_ge(hi_done, u * QKM + m + 1)
                            dve.tensor_tensor(rest[:, m, :], ps_qk[:, m % 2, :], parts[:, c, m, 0, :],
                                              ALU.subtract).then_inc(rest_done, 1)

                turn(0)
                with dve.Fori(1, BATCH) as b:
                    turn(b)

            @block.scalar
            def _(act):
                act.wait_ge(ones_done, 1)
                def turn(b):
                    for c in range(CHUNKS):
                        u = b * CHUNKS + c
                        act.wait_ge(xt_made, u + 1)
                        act.activation(x_t[:, c, :, :], ps_t[:, :, :], ACT.Copy).then_inc(xt_kept, 1)
                        act.wait_ge(parts_stored[c], 16 * QKM * b)
                        act.wait_ge(v_stored[c], 16 * b)
                        for m in range(QKM):
                            act.wait_ge(qk_made, u * QKM + m + 1)
                            act.activation(parts[:, c, m, 0, :], ps_qk[:, m % 2, :], ACT.Copy)\
                               .then_inc(hi_done, 1)
                            act.wait_ge(rest_done, u * QKM + m + 1)
                            act.activation(parts[:, c, m, 1, :], rest[:, m, :], ACT.Copy)\
                               .then_inc(mid_done, 1)
                        for r in range(2):
                            act.wait_ge(v_made, 2 * u + r + 1)
                            act.activation(v_sb[:, c, 2 * r:2 * r + 2, :, 0:HD],
                                           ps_v[:, r, :, :].rearrange("p t (n h) -> p t n h", h=HD),
                                           ACT.Copy).then_inc(v_kept, 1)

                turn(0)
                with act.Fori(1, BATCH) as b:
                    turn(b)

            @block.tensor
            def _(pe):
                pe.wait_ge(ident_done, 2)
                pe.wait_ge(w_packed, 3 * KC)
                def turn(b):
                    for c in range(CHUNKS):
                        u = b * CHUNKS + c
                        pe.wait_ge(x_loaded[c], 16 * b + 16)
                        pe.wait_ge(xt_kept, u)
                        for k in range(KC):
                            for t in range(CT):
                                last = pe.transpose(ps_t[:, k, t * P:(t + 1) * P],
                                                    x_rows[:, c, t, k * P:(k + 1) * P], ident[:, :])
                        last.then_inc(xt_made, 1)
                        pe.wait_ge(xt_kept, u + 1)
                        for m in range(QKM):
                            pe.wait_ge(rest_done, u * QKM + max(m - 1, 0))
                            for k in range(KC):
                                last = pe.matmul(ps_qk[:, m % 2, :], wqk[:, k, m, :], x_t[:, c, k, :],
                                                 start=(k == 0), stop=(k == KC - 1))
                            last.then_inc(qk_made, 1)
                        pe.wait_ge(v_kept, 2 * u)
                        for r in range(2):
                            for t in range(2):
                                for k in range(KC):
                                    s = (2 * r + t) * P
                                    last = pe.matmul(ps_v[:, r, t, :], x_t[:, c, k, s:s + P], wv[:, k, :],
                                                     start=(k == 0), stop=(k == KC - 1))
                            last.then_inc(v_made, 1)

                turn(0)
                with pe.Fori(1, BATCH) as b:
                    turn(b)


def attend(nc, qk_parts, v_rows, heads_out):
    with ExitStack() as ctx:
        def sb(name, shape, dt):
            return ctx.enter_context(nc.sbuf_tensor(name, shape, dt))

        def pb(name, shape, dt):
            return ctx.enter_context(nc.psum_tensor(name, shape, dt))

        def sem(name):
            return ctx.enter_context(nc.semaphore(name))

        STEPS = [(c, kt) for c in range(CHUNKS) for kt in range(CT * (c + 1))]
        NST = len(STEPS)
        PIECES = [(h, qt, s, min((qt + 1) * P - s, CHUNK), s // CHUNK)
                  for h in range(QUAD) for qt in range(TILES) for s in range(0, (qt + 1) * P, CHUNK)]
        NPC = len(PIECES)
        WIDTHS = [min(CHUNK, (c + 1) * CHUNK - kt * P) for c, kt in STEPS]
        ENDS = []
        for st in range(NST):
            due = sum(p[3] for p in PIECES) * sum(WIDTHS[:st + 1]) // sum(WIDTHS)
            ENDS.append(sum(sum(p[3] for p in PIECES[:i + 1]) <= due for i in range(NPC)))
        SHARE = [range(a, b) for a, b in zip([0] + ENDS, ENDS)]
        PB = 3
        BANKS = 3
        assert NPC % BANKS == 0 and QUAD * NST % BANKS == 0
        LOADS = 16 * (2 * len(TERMS) + 1)

        qs = sb("a_qs", [P, QUADS, QUAD, SEQ], BF16)
        ks = sb("a_ks", [P, QUADS, QUAD, SEQ], BF16)
        vq = sb("a_vq", [P, QUADS, TILES, QUAD, VW], F32)
        probs = sb("a_probs", [P, PB, QUAD, CHUNK], F32)
        ident = sb("a_ident", [P, P], F32)
        ident16 = sb("a_ident16", [P, P], BF16)
        mask16 = sb("a_mask16", [P, P], BF16)
        pick = sb("a_pick", [P, QUAD], F32)
        o_sb = sb("a_o_sb", [P, 2, CHUNK], F32)
        inv = sb("a_inv", [P, 2, CT, QUAD], F32)
        out_sb = sb("a_out_sb", [P, 2, 64, SEQ // 64], F32)
        wide = sb("a_wide", [P, CT, QUAD, VW], F32)
        mx = sb("a_mx", [P, 2, 2, QUAD, TILES], F32)
        mrow = sb("a_mrow", [QUAD * TILES, PARTS, P], BF16)
        mrest = sb("a_mrest", [QUAD * TILES, P], F32)
        ps_s = pb("a_ps_s", [P, BANKS, CHUNK], F32)
        ps_m = pb("a_ps_m", [P, BANKS, CHUNK], F32)
        ps_o = pb("a_ps_o", [P, CHUNK], F32)
        ps_x = pb("a_ps_x", [P, CHUNK], F32)

        ident_done = sem("a_ident_done")
        const_done = sem("a_const_done")
        ones_done = sem("a_ones_done")
        loaded = [sem(f"a_loaded{j}") for j in range(QUADS)]
        rows_made = sem("a_rows_made")
        rows_max = sem("a_rows_max")
        max_done = sem("a_max_done")
        max_t = sem("a_max_t")
        max_split = sem("a_max_split")
        max_sent = sem("a_max_sent")
        scores = sem("a_scores")
        exps = [sem(f"a_exps{e}") for e in range(2)]
        mask_turn = sem("a_mask_turn")
        masked = sem("a_masked")
        pv_done = sem("a_pv_done")
        o_kept = sem("a_o_kept")
        sums_made = sem("a_sums_made")
        wide_done = sem("a_wide_done")
        inv_t = sem("a_inv_t")
        inv_done = sem("a_inv_done")
        out_done = sem("a_out_done")
        out_sent = [sem(f"a_out_sent{e}") for e in range(2)]

        def part(share, g):
            n = len(share)
            at = [min(int(8 * (i + 0.5) / n), QUAD) for i in range(n)]
            return [i for i, a in zip(share, at) if a == g]

        def step_shape(st):
            c, kt = STEPS[st]
            off = max(kt * P - c * CHUNK, 0)
            return off, CHUNK - off

        with nc.Block() as block:
            @block.sync
            def _(sp):
                def load(b, j):
                    for i, (pq, pk) in enumerate(TERMS):
                        for dst, first, part in ((qs, 0, pq), (ks, HEADS * HD, pk)):
                            r = first + j * QUAD * HD
                            sp.dma_start(dst[i * HD:(i + 1) * HD, j, :, :],
                                         qk_parts[b, r:r + QUAD * HD, part, :]
                                         .rearrange("(n h) s -> h n s", h=HD)).then_inc(loaded[j], 16)
                    sp.dma_start(vq[:, j, :, :, :].rearrange("p t n v -> p t (n v)"),
                                 v_rows[b, :, :, j * QUAD * VW:(j + 1) * QUAD * VW].rearrange("t p v -> p t v"))\
                        .then_inc(loaded[j], 16)

                def send_max(t, j):
                    sp.wait_ge(max_split, 4 * t + 4)
                    for i in range(PARTS):
                        sp.dma_start(qs[TROWS + i:TROWS + i + 1, j, :, :]
                                     .rearrange("o n (t q) -> o (n t) q", q=P),
                                     mrow[:, i, :]).then_inc(max_sent, 16)

                def send_out(b, j):
                    sp.wait_ge(out_done, CHUNKS * (QUADS * b + j + 1))
                    for n in range(QUAD):
                        dst = heads_out[b].rearrange("(r h) (n i) -> n h r i", h=HD, i=SEQ // 64)
                        sp.dma_start(dst[j * QUAD + n], out_sb[n * VW:n * VW + HD, j % 2, :, :])\
                            .then_inc(out_sent[j % 2], 16)

                def turn(b, last):
                    for j in range(QUADS):
                        t = QUADS * b + j
                        if not (last and j == QUADS - 1):
                            send_max(t + 1, (j + 1) % QUADS)
                        if not (isinstance(t, int) and t == 0):
                            before, jb = (b, j - 1) if j else (b - 1, QUADS - 1)
                            if not (last and j):
                                sp.wait_ge(pv_done, NST * t)
                                load(before + 1, jb)
                            send_out(before, jb)

                for j in range(QUADS):
                    load(0, j)
                send_max(0, 0)
                turn(0, False)
                with sp.Fori(1, BATCH - 1) as b:
                    turn(b, False)
                turn(BATCH - 1, True)
                send_out(BATCH - 1, QUADS - 1)
                for e in range(2):
                    sp.wait_ge(out_sent[e], 16 * QUAD * SLOTS // 2)

            @block.gpsimd
            def _(pool):
                identity(pool, ident, ident_done)
                pool.memset(mask16[:, :], 0.0).then_inc(const_done, 1)
                pool.memset(pick[:, :], 0.0).then_inc(const_done, 1)
                pool.wait_ge(const_done, 2)
                pool.affine_select(out=mask16[:, :], in_=mask16[:, :], compare_op=ALU.is_ge, fill=NEG,
                                   base=0, pattern=[[-1, P]], channel_multiplier=1).then_inc(const_done, 1)
                pool.affine_select(out=pick[:, :], in_=pick[:, :], compare_op=ALU.not_equal, fill=1.0,
                                   base=-HD, pattern=[[-VW, QUAD]], channel_multiplier=1).then_inc(const_done, 1)
                pool.wait_ge(ident_done, 2)
                pool.tensor_copy(ident16[:, :], ident[:, :]).then_inc(const_done, 1)
                def turn(b):
                    for j in range(QUADS):
                        t = QUADS * b + j
                        n = 0
                        for st, (c, kt) in enumerate(STEPS):
                            if kt < c * CT:
                                continue
                            n += 1
                            pool.wait_ge(exps[1], 2 * (NST * t + st + 1))
                            pool.sem_inc(mask_turn, 1)
                            tile = probs[:, st % PB, :, 0:P]
                            pool.affine_select(out=tile, in_=tile, compare_op=ALU.is_ge, fill=0.0, base=0,
                                               pattern=[[0, QUAD], [1, P]], channel_multiplier=-1)\
                                .then_inc(masked, 1)

                turn(0)
                with pool.Fori(1, BATCH) as b:
                    turn(b)

            @block.scalar
            def _(act):
                def keep_o(t, c):
                    act.wait_ge(pv_done, NST * t + (CT if c == 0 else NST))
                    if not (isinstance(t, int) and t == 0):
                        act.wait_ge(out_done, CHUNKS * (t - 1) + c + 1)
                    act.activation(o_sb[:, c, :], ps_o[:, :], ACT.Copy).then_inc(o_kept, 1)

                def widen(t, c):
                    act.wait_ge(inv_done, CHUNKS * t + c + 1)
                    act.activation(wide[:, :, :, :],
                                   inv[:, c, :, :].rearrange("p t (n o) -> p t n o", o=1)
                                   .broadcast_to((P, CT, QUAD, VW)), ACT.Copy).then_inc(wide_done, 1)

                def turn(b):
                    for j in range(QUADS):
                        t = QUADS * b + j
                        for st, (c, kt) in enumerate(STEPS):
                            off, width = step_shape(st)
                            if st >= PB or not (isinstance(t, int) and t == 0):
                                act.wait_ge(pv_done, NST * t + st - PB + 1)
                            for h in range(QUAD):
                                n = QUAD * st + h
                                act.wait_ge(scores, QUAD * NST * t + n + 1)
                                act.activation(probs[:, st % PB, h, 0:width], ps_s[:, n % BANKS, 0:width],
                                               ACT.Exp, scale=SCALE).then_inc(exps[h % 2], 1)
                            if st == 0 and not (isinstance(t, int) and t == 0):
                                keep_o(t - 1, 1)
                            if st == 3 and not (isinstance(t, int) and t == 0):
                                widen(t - 1, 1)
                            if st == CT:
                                keep_o(t, 0)
                            if st == CT + 3:
                                widen(t, 0)

                turn(0)
                with act.Fori(1, BATCH) as b:
                    turn(b)
                keep_o(SLOTS - 1, 1)
                widen(SLOTS - 1, 1)

            @block.vector
            def _(dve):
                def take_max(v, e, i):
                    h, qt, s, width, half = PIECES[i]
                    dve.wait_ge(rows_made, NPC * v + i + 1)
                    dve.tensor_reduce(mx[:, e, half, h, qt:qt + 1], ps_m[:, i % BANKS, 0:width],
                                      AX_X, ALU.max).then_inc(rows_max, 1)

                def join_max(v, e):
                    dve.wait_ge(rows_max, NPC * (v + 1))
                    dve.tensor_tensor(mx[:, e, 0, :, CT:TILES], mx[:, e, 0, :, CT:TILES],
                                      mx[:, e, 1, :, CT:TILES], ALU.max).then_inc(max_done, 1)

                def split_max(v):
                    dve.wait_ge(max_t, v + 1)
                    src = ps_x[0:QUAD * TILES, 0:P]
                    dve.wait_ge(max_sent, 16 * PARTS * v)
                    dve.tensor_scalar(mrow[:, 0, :], src, -1.0, None, ALU.mult).then_inc(max_split, 1)
                    dve.wait_ge(max_split, 4 * v + 1)
                    dve.scalar_tensor_tensor(out=mrest[:, :], in0=src, scalar=-1.0, in1=mrow[:, 0, :],
                                             op0=ALU.mult, op1=ALU.subtract).then_inc(max_split, 1)
                    dve.wait_ge(max_split, 4 * v + 2)
                    dve.tensor_copy(mrow[:, 1, :], mrest[:, :]).then_inc(max_split, 1)
                    dve.wait_ge(max_split, 4 * v + 3)
                    dve.tensor_tensor(mrow[:, 2, :], mrest[:, :], mrow[:, 1, :], ALU.subtract)\
                       .then_inc(max_split, 1)

                def invert(t, c):
                    dve.wait_ge(sums_made, CHUNKS * t + c + 1)
                    dve.reciprocal(inv[:, c, :, :],
                                   ps_x[:, 0:CT * QUAD].rearrange("p (t n) -> p t n", n=QUAD))\
                       .then_inc(inv_done, 1)

                def form_out(b, j, c):
                    t, e = QUADS * b + j, j % 2
                    dve.wait_ge(inv_t, CHUNKS * t + c + 1)
                    dve.wait_ge(out_sent[e], 16 * QUAD * (QUADS // 2 * b + j // 2))
                    dve.tensor_tensor(out_sb[:, e, :, 8 * c:8 * c + 8].rearrange("p r i -> p i r"),
                                      ps_x[:, :].rearrange("p (i r) -> p i r", r=64),
                                      o_sb[:, c, :].rearrange("p (i r) -> p i r", r=64), ALU.mult)\
                       .then_inc(out_done, 1)

                for j in range(QUADS):
                    dve.memset(ks[TROWS:P, j, :, :], 1.0).then_inc(ones_done, 1)
                for v in range(2):
                    for i in range(NPC):
                        take_max(v, v, i)
                    if v == 0:
                        join_max(v, v)
                        split_max(v)

                def turn(b, last):
                    for j in range(QUADS):
                        t = QUADS * b + j
                        more = not (last and j + 2 >= QUADS)
                        after = not (last and j == QUADS - 1)
                        before = not (isinstance(t, int) and t == 0)
                        if after:
                            join_max(t + 1, (j + 1) % 2)
                        for st in range(NST):
                            if more:
                                for i in SHARE[st]:
                                    take_max(t + 2, j % 2, i)
                            if st == 1 and after:
                                split_max(t + 1)
                            if before and st == 2:
                                invert(t - 1, 1)
                            if before and st == 4:
                                form_out(*((b, j - 1) if j else (b - 1, QUADS - 1)), 1)
                            if st == CT + 2:
                                invert(t, 0)
                            if st == CT + 4:
                                form_out(b, j, 0)

                turn(0, False)
                with dve.Fori(1, BATCH - 1) as b:
                    turn(b, False)
                turn(BATCH - 1, True)
                invert(SLOTS - 1, 1)
                form_out(BATCH - 1, QUADS - 1, 1)

            @block.tensor
            def _(pe):
                pe.wait_ge(const_done, 5)
                pe.wait_ge(ones_done, QUADS)

                def rows(v, j, i):
                    h, qt, s, width, half = PIECES[i]
                    if i >= BANKS or not (isinstance(v, int) and v == 0):
                        pe.wait_ge(rows_max, NPC * v + i - BANKS + 1)
                    out = ps_m[:, i % BANKS, :]
                    own = s + width == (qt + 1) * P
                    last = pe.matmul(out[:, 0:width], qs[0:TROWS, j, h, qt * P:(qt + 1) * P],
                                     ks[0:TROWS, j, h, s:s + width], start=True, stop=not own)
                    if own:
                        last = pe.matmul(out[:, width - P:width], ident16[:, :], mask16[:, :],
                                         start=False, stop=True)
                    last.then_inc(rows_made, 1)

                def turn_max(v, e):
                    pe.wait_ge(max_done, v + 1)
                    pe.transpose(ps_x[0:QUAD * TILES, 0:P], mx[:, e, 0, :, :].rearrange("p n t -> p (n t)"),
                                 ident[:, :]).then_inc(max_t, 1)

                for v in range(2):
                    pe.wait_ge(loaded[v], LOADS)
                    for i in range(NPC):
                        rows(v, v, i)
                    if v == 0:
                        turn_max(v, v)

                def products(t, j, st):
                    c, kt = STEPS[st]
                    off, width = step_shape(st)
                    pe.wait_ge(exps[1], 2 * (NST * t + st + 1))
                    if kt >= c * CT:
                        own = sum(k >= cc * CT for cc, k in STEPS[:st + 1])
                        pe.wait_ge(masked, TILES * t + own)
                    if kt == 0:
                        pe.wait_ge(o_kept, CHUNKS * t + c)
                    for h in range(QUAD):
                        last = pe.matmul(ps_o[h * VW:(h + 1) * VW, off:CHUNK], vq[:, j, kt, h, :],
                                         probs[:, st % PB, h, 0:width],
                                         start=(kt == 0), stop=(kt == CT * (c + 1) - 1))
                    last.then_inc(pv_done, 1)

                def sums(t, c):
                    pe.wait_ge(o_kept, CHUNKS * t + c + 1)
                    for q in range(CT):
                        s = pe.matmul(ps_x[:, q * QUAD:(q + 1) * QUAD], o_sb[:, c, q * P:(q + 1) * P],
                                      pick[:, :], start=True, stop=True)
                    s.then_inc(sums_made, 1)

                def turn_inv(t, c):
                    pe.wait_ge(wide_done, CHUNKS * t + c + 1)
                    for q in range(CT):
                        s = pe.transpose(ps_x[:, q * P:(q + 1) * P], wide[:, q, :, :].rearrange("p n v -> p (n v)"),
                                         ident[:, :])
                    s.then_inc(inv_t, 1)

                def turn(b, last):
                    for j in range(QUADS):
                        t = QUADS * b + j
                        more = not (last and j + 2 >= QUADS)
                        after = not (last and j == QUADS - 1)
                        before = not (isinstance(t, int) and t == 0)
                        jm = (j + 2) % QUADS
                        pe.wait_ge(max_sent, 16 * PARTS * (t + 1))
                        if more:
                            pe.wait_ge(loaded[jm], LOADS * (b + 1 + (j + 2) // QUADS))
                        for st, (c, kt) in enumerate(STEPS):
                            off, width = step_shape(st)
                            q0 = c * CHUNK + off
                            for h in range(QUAD):
                                n = QUAD * st + h
                                if before or n >= BANKS:
                                    pe.wait_ge(exps[(n - BANKS) % 2], 2 * NST * t + (n - BANKS) // 2 + 1)
                                pe.matmul(ps_s[:, n % BANKS, 0:width], ks[0:MROWS, j, h, kt * P:(kt + 1) * P],
                                          qs[0:MROWS, j, h, q0:q0 + width], start=True, stop=True)\
                                  .then_inc(scores, 1)
                                if more:
                                    for i in part(SHARE[st], h):
                                        rows(t + 2, jm, i)
                            if st >= 1:
                                products(t, j, st - 1)
                            elif before:
                                products(t - 1, (j - 1) % QUADS, NST - 1)
                            if more:
                                for i in part(SHARE[st], QUAD):
                                    rows(t + 2, jm, i)
                            if st == 1 and after:
                                pe.wait_ge(out_done, CHUNKS * t - 1 if before else 0)
                                turn_max(t + 1, (j + 1) % 2)
                            if before and st == 2:
                                if after:
                                    pe.wait_ge(max_split, 4 * (t + 2))
                                else:
                                    pe.wait_ge(out_done, CHUNKS * t - 1)
                                sums(t - 1, 1)
                            if before and st == 4:
                                turn_inv(t - 1, 1)
                            if st == CT + 2:
                                pe.wait_ge(out_done, CHUNKS * t)
                                if not before:
                                    pe.wait_ge(max_split, 4 * (t + 2))
                                sums(t, 0)
                            if st == CT + 4:
                                turn_inv(t, 0)

                turn(0, False)
                with pe.Fori(1, BATCH - 1) as b:
                    turn(b, False)
                turn(BATCH - 1, True)
                products(SLOTS - 1, QUADS - 1, NST - 1)
                pe.wait_ge(out_done, CHUNKS * SLOTS - 1)
                sums(SLOTS - 1, 1)
                turn_inv(SLOTS - 1, 1)


def feed(nc, x, heads_out, w_out, mix_kernel, w1, b1, w2, b2, wo1, bo1, wo2, bo2, gamma, beta, out):
    with ExitStack() as ctx:
        def sb(name, shape, dt):
            return ctx.enter_context(nc.sbuf_tensor(name, shape, dt))

        def pb(name, shape, dt):
            return ctx.enter_context(nc.psum_tensor(name, shape, dt))

        def sem(name):
            return ctx.enter_context(nc.semaphore(name))

        PATHS, _, DM = w1.shape
        MC = (PATHS + 1) * DM // P
        LAST = MC - 1
        EPS = 1e-5
        X2 = DM + PATHS

        w1_sb = sb("f_w1", [P, KC, PATHS + 1, DM], F32)
        w2_sb = sb("f_w2", [P, MC, D], F32)
        wo2_sb = sb("f_wo2", [P, PATHS], F32)
        bias = sb("f_bias", [P, MC], F32)
        mixk = sb("f_mixk", [P, 3, KC], F32)
        wout_sb = sb("f_wout", [P, HEADS * HD // P, D], F32)
        row = sb("f_row", [1, 2 * D + PATHS], F32)
        ones = sb("f_ones", [P, P], F32)
        wsum = sb("f_wsum", [P, D], F32)
        gb = sb("f_gb", [P, 2, D], F32)
        bo2_sb = sb("f_bo2", [P, PATHS], F32)
        prio = sb("f_prio", [P, PATHS], F32)
        ident = sb("f_ident", [P, P], F32)
        ident16 = sb("f_ident16", [P, P], BF16)
        widen = sb("f_widen", [P, PATHS + 1, DM], BF16)
        half = sb("f_half", [P, TILES], F32)

        x_in = sb("f_x_in", [P, TILES, D], F32)
        a_in = sb("f_a_in", [P, TILES, D], F32)
        aw = sb("f_aw", [P, TILES, D], F32)
        x1 = sb("f_x1", [P, 2, TILES, D], F32)
        x1_t = sb("f_x1_t", [P, KC, SEQ + 2], F32)
        xm = sb("f_xm", [P, 2, KC, SEQ], F32)
        mixa = sb("f_mixa", [P, 2, SEQ], F32)
        st_a = sb("f_st_a", [P, TILES, 6], F32)
        mv_a = sb("f_mv_a", [P, TILES, 2], F32)
        ve_a = sb("f_ve_a", [P, TILES], F32)
        rs_a = sb("f_rs_a", [P, TILES], F32)

        hid = sb("f_hid", [P, MC, CHUNK], F32)
        hm = sb("f_hm", [P, MC, CHUNK], F32)
        sc = sb("f_sc", [P, CT, PATHS], F32)
        eq = sb("f_eq", [P, CT, PATHS], F32)
        best = sb("f_best", [P, 2, CT], F32)
        pick = sb("f_pick", [P, CT, PATHS], BF16)
        pick_t = sb("f_pick_t", [P, CHUNK], BF16)
        y = sb("f_y", [P, CT, D], F32)
        z = sb("f_z", [P, CT, D], F32)
        xb = sb("f_xb", [P, CT, D], F32)
        st_b = sb("f_st_b", [P, CT, 6], F32)
        mv_b = sb("f_mv_b", [P, CT, 2], F32)
        ve_b = sb("f_ve_b", [P, CT], F32)
        rs_b = sb("f_rs_b", [P, 2, CT], F32)
        res = sb("f_res", [P, 2, CT, D], F32)

        ps_t = pb("f_ps_t", [P, 2, CHUNK], F32)
        ps_h = pb("f_ps_h", [P, 2, CHUNK], F32)
        ps_k = pb("f_ps_k", [P, CHUNK], F32)
        ps_o = pb("f_ps_o", [P, 2, 2, D], F32)
        ps_c = pb("f_ps_c", [P, CHUNK], F32)
        ps_pick = ps_c[:, CHUNK // 2:CHUNK].bitcast(BF16)

        w_loaded = sem("f_w_loaded")
        const_done = sem("f_const_done")
        pool_const = sem("f_pool_const")
        bcast_made = sem("f_bcast_made")
        bcast_kept = sem("f_bcast_kept")
        in_loaded = sem("f_in_loaded")
        in_used = sem("f_in_used")
        aw_done = sem("f_aw_done")
        ve_done = sem("f_ve_done")
        rs_done = sem("f_rs_done")
        x1_done = sem("f_x1_done")
        xt_made = sem("f_xt_made")
        xt_kept = sem("f_xt_kept")
        xm_done = sem("f_xm_done")
        chain = sem("f_chain")
        h_made = sem("f_h_made")
        h_kept = sem("f_h_kept")
        sc_made = sem("f_sc_made")
        picked = sem("f_picked")
        pick_made = sem("f_pick_made")
        pick_kept = sem("f_pick_kept")
        k_made = sem("f_k_made")
        hm_done = sem("f_hm_done")
        o_made = sem("f_o_made")
        y_done = sem("f_y_done")
        xb_done = sem("f_xb_done")
        carrier = sem("f_carrier")
        res_done = sem("f_res_done")
        stored = sem("f_stored")

        def turns(eng, turn):
            for e in range(2):
                turn(e, e, False)
            with eng.Fori(1, BATCH // 2 - 1) as pair:
                for e in range(2):
                    turn(2 * pair + e, e, False)
            for e in range(2):
                turn(BATCH - 2 + e, e, e == 1)

        with nc.Block() as block:
            @block.sync
            def _(sp):
                def load_in(b):
                    sp.dma_start(x_in[:, :, :], x[b].rearrange("(t p) d -> p t d", p=P)).then_inc(in_loaded, 16)
                    sp.dma_start(a_in[:, :, :], heads_out[b].rearrange("(t p) d -> p t d", p=P))\
                        .then_inc(in_loaded, 16)

                load_in(0)
                sp.dma_start(wout_sb[:, :, :], w_out.rearrange("(a n) h d -> (n h) a d", n=P // HD))\
                    .then_inc(w_loaded, 16)
                for i, v in enumerate((gamma, beta)):
                    sp.dma_start(row[:, i * D:(i + 1) * D], v.rearrange("(a d) -> a d", a=1)).then_inc(w_loaded, 16)
                sp.dma_start(row[:, 2 * D:2 * D + PATHS], bo2.rearrange("(a d) -> a d", a=1)).then_inc(w_loaded, 16)
                for k in range(KC):
                    rows = slice(k * P, (k + 1) * P)
                    sp.dma_start(w1_sb[:, k, 0:PATHS, :], w1[:, rows, :].rearrange("p d m -> d p m"))\
                        .then_inc(w_loaded, 16)
                    sp.dma_start(w1_sb[:, k, PATHS, :], wo1[rows, :]).then_inc(w_loaded, 16)
                    sp.dma_start(mixk[:, :, k], mix_kernel[:, rows].rearrange("t d -> d t"),
                                 allow_slow_non_contiguous=True).then_inc(w_loaded, 16)
                for m in range(LAST):
                    sp.dma_start(w2_sb[:, m, :], w2[2 * m:2 * m + 2].rearrange("q m d -> (q m) d"))\
                        .then_inc(w_loaded, 16)
                    sp.dma_start(bias[:, m:m + 1],
                                 b1[2 * m:2 * m + 2].rearrange("q (m o) -> (q m) o", o=1)).then_inc(w_loaded, 16)
                sp.dma_start(w2_sb[0:DM, LAST, :], w2[PATHS - 1]).then_inc(w_loaded, 16)
                sp.dma_start(w2_sb[DM:X2, LAST, :], b2).then_inc(w_loaded, 16)
                sp.dma_start(bias[0:DM, LAST:MC], b1[PATHS - 1].rearrange("(m o) -> m o", o=1)).then_inc(w_loaded, 16)
                sp.dma_start(bias[DM:P, LAST:MC], bo1.rearrange("(m o) -> m o", o=1)).then_inc(w_loaded, 16)
                sp.dma_start(wo2_sb[DM:P, :], wo2).then_inc(w_loaded, 16)

                def turn(b, e, last):
                    if not last:
                        sp.wait_ge(in_used, b + 1)
                        load_in_next(b + 1)
                    for c in range(CHUNKS):
                        n = CHUNKS * b + c
                        sp.wait_ge(res_done, n + 1)
                        sp.dma_start(out[b].rearrange("(t p) d -> p t d", p=P)[:, c * CT:(c + 1) * CT, :],
                                     res[:, c, :, :]).then_inc(stored, 16)

                load_in_next = load_in
                turns(sp, turn)
                sp.wait_ge(stored, 16 * CHUNKS * BATCH)

            WL = 16 * (4 + 3 * KC + 2 * LAST + 5)

            @block.gpsimd
            def _(pool):
                identity(pool, ident, const_done)
                pool.memset(ones[:, :], 1.0).then_inc(pool_const, 1)
                pool.memset(widen[:, :, :], 0.0).then_inc(pool_const, 1)
                pool.memset(half[:, :], -0.5).then_inc(pool_const, 1)
                pool.memset(pick_t[:, :], 0.0).then_inc(pool_const, 1)
                for k in range(KC):
                    pool.memset(x1_t[:, k, 0:SEQ + 2:SEQ + 1], 0.0).then_inc(pool_const, 1)
                for p in range(PATHS):
                    pool.memset(prio[:, p:p + 1], float(PATHS - p)).then_inc(pool_const, 1)
                pool.wait_ge(const_done, 2)
                pool.tensor_copy(ident16[:, :], ident[:, :]).then_inc(pool_const, 1)
                pool.wait_ge(pool_const, 5 + KC + PATHS)
                pool.affine_select(out=widen[:, :, :], in_=widen[:, :, :], compare_op=ALU.not_equal, fill=1.0,
                                   base=0, pattern=[[-1, PATHS + 1], [0, DM]], channel_multiplier=1)\
                    .then_inc(pool_const, 1)
                pool.wait_ge(bcast_kept, 4)

                def rsqrt(count, ve, rs, k):
                    pool.wait_ge(ve_done, count)
                    pool.tensor_tensor(rs, ve, half[:, 0:k], ALU.pow).then_inc(rs_done, 1)

                def stage_a(b, before):
                    pool.wait_ge(x1_done, b)
                    pool.wait_ge(in_loaded, 32 * (b + 1))
                    pool.tensor_tensor(aw[:, :, :], a_in[:, :, :],
                                       wsum[:, :].rearrange("p (o d) -> p o d", o=1).broadcast_to((P, TILES, D)),
                                       ALU.mult).then_inc(aw_done, 1)
                    rsqrt(before + 1, ve_a[:, :], rs_a[:, :], TILES)

                def turn(b, e, last):
                    for c in range(CHUNKS):
                        n = CHUNKS * b + c
                        if c == 0 and not last:
                            stage_a(b + 1, 1 + 5 * b)
                        base = 5 * b + (2 if not last else 1) + 2 * c
                        pool.wait_ge(res_done, n)
                        pool.wait_ge(x1_done, b + 1)
                        pool.tensor_tensor(xb[:, :, :], x1[:, e, c * CT:(c + 1) * CT, :],
                                           gb[:, 1, :].rearrange("p (o d) -> p o d", o=1).broadcast_to((P, CT, D)),
                                           ALU.add).then_inc(xb_done, 1)
                        for i in range(2):
                            rsqrt(base + i + 1, ve_b[:, :], rs_b[:, i, :], CT)

                stage_a(0, 0)
                turns(pool, turn)

            @block.scalar
            def _(act):
                act.wait_ge(bcast_made, 1)
                act.activation(wsum[:, :], ps_o[:, 0, 0, :], ACT.Copy).then_inc(bcast_kept, 1)
                for i in range(2):
                    act.wait_ge(bcast_made, i + 2)
                    act.activation(gb[:, i, :], ps_h[:, i, 0:D], ACT.Copy).then_inc(bcast_kept, 1)
                act.wait_ge(bcast_made, 4)
                act.activation(bo2_sb[:, :], ps_c[:, 0:PATHS], ACT.Copy).then_inc(bcast_kept, 1)
                act.wait_ge(w_loaded, WL)

                def stage_a(b):
                    act.wait_ge(xm_done, b)
                    for g in range(CHUNKS):
                        for k in range(KC):
                            act.wait_ge(xt_made, 4 * b + 2 * g + k + 1)
                            act.activation(x1_t[:, k, 1 + g * CHUNK:1 + (g + 1) * CHUNK], ps_t[:, k, :],
                                           ACT.Copy).then_inc(xt_kept, 1)

                def turn(b, e, last):
                    for c in range(CHUNKS):
                        n = CHUNKS * b + c
                        act.wait_ge(hm_done, MC * n)
                        act.wait_ge(h_made, MC * n + 1)
                        act.activation(hid[DM:P, LAST, :], ps_h[DM:P, 0, :], ACT.Tanh,
                                       bias=bias[DM:P, LAST:MC]).then_inc(h_kept, 1)
                        act.activation(hid[0:DM, LAST, :], ps_h[0:DM, 0, :], ACT.Identity,
                                       bias=bias[0:DM, LAST:MC]).then_inc(h_kept, 1)
                        for m in range(LAST):
                            act.wait_ge(h_made, MC * n + m + 2)
                            act.activation(hid[:, m, :], ps_h[:, (m + 1) % 2, :], ACT.Identity,
                                           bias=bias[:, m:m + 1]).then_inc(h_kept, 1)
                        act.wait_ge(pick_made, n + 1)
                        act.activation(pick_t[0:PATHS, :], ps_pick[0:PATHS, :], ACT.Copy).then_inc(pick_kept, 1)
                        act.wait_ge(o_made, 2 * n)
                        act.activation(hm[DM:X2, LAST, :], ps_pick[0:PATHS, :], ACT.Copy).then_inc(pick_kept, 1)
                        if c == 0 and not last:
                            stage_a(b + 1)

                stage_a(0)
                turns(act, turn)

            @block.vector
            def _(dve):
                dve.wait_ge(bcast_kept, 4)
                dve.wait_ge(w_loaded, WL)
                links = [0]

                def link(ins, turn):
                    base, total = turn
                    links[0] += 1
                    ins.then_inc(chain, 1)
                    dve.wait_ge(chain, base + links[0])

                def statistics(src, tiles, st, mv, ve, at):
                    for i in range(tiles):
                        ins = dve.bn_stats(st[:, i, :], src[:, i, :])
                    link(ins, at)
                    dve.sem_inc(carrier, 1)
                    for i in range(tiles):
                        ins = dve.bn_aggr(mv[:, i, :], st[:, i, :])
                    link(ins, at)
                    dve.tensor_scalar(ve, mv[:, :, 1], EPS, None, ALU.add).then_inc(ve_done, 1)

                def layernorm(b, e, at):
                    dve.wait_ge(in_loaded, 32 * (b + 1))
                    dve.wait_ge(aw_done, b + 1)
                    ins = dve.tensor_tensor(aw[:, :, :], aw[:, :, :], x_in[:, :, :], ALU.add)
                    ins.then_inc(in_used, 1)
                    dve.wait_ge(in_used, b + 1)
                    dve.sem_inc(carrier, 1)
                    statistics(aw, TILES, st_a, mv_a, ve_a[:, :], at)

                def normalize(b, e, count):
                    dve.wait_ge(rs_done, count)
                    for i in range(TILES):
                        ins = dve.tensor_scalar(x1[:, e, i, :], aw[:, i, :], mv_a[:, i, 0:1], rs_a[:, i:i + 1],
                                                ALU.subtract, ALU.mult)
                    ins.then_inc(x1_done, 1)

                def mix(b, e, at):
                    dve.wait_ge(xt_kept, 4 * (b + 1))
                    for k in range(KC):
                        link(dve.tensor_scalar(mixa[:, 0, :], x1_t[:, k, 0:SEQ], mixk[:, 0, k:k + 1], None,
                                               ALU.mult), at)
                        link(dve.scalar_tensor_tensor(out=mixa[:, 1, :], in0=x1_t[:, k, 1:SEQ + 1],
                                                      scalar=mixk[:, 1, k:k + 1], in1=mixa[:, 0, :],
                                                      op0=ALU.mult, op1=ALU.add), at)
                        ins = dve.scalar_tensor_tensor(out=xm[:, e, k, :], in0=x1_t[:, k, 2:SEQ + 2],
                                                       scalar=mixk[:, 2, k:k + 1], in1=mixa[:, 1, :],
                                                       op0=ALU.mult, op1=ALU.add)
                        if k < KC - 1:
                            link(ins, at)
                    ins.then_inc(xm_done, 1)

                def choose(n, at):
                    dve.wait_ge(sc_made, n + 1)
                    link(dve.tensor_tensor(sc[:, :, :],
                                           ps_c[:, 0:CT * PATHS].rearrange("p (t q) -> p t q", q=PATHS),
                                           bo2_sb[:, :].rearrange("p (o q) -> p o q", o=1).broadcast_to((P, CT, PATHS)),
                                           ALU.add), at)
                    link(dve.tensor_reduce(best[:, 0, :], sc[:, :, :], AX_X, ALU.max), at)
                    link(dve.tensor_tensor(eq[:, :, :], sc[:, :, :],
                                           best[:, 0, :].rearrange("p (t o) -> p t o", o=1).broadcast_to((P, CT, PATHS)),
                                           ALU.is_equal), at)
                    link(dve.tensor_tensor(sc[:, :, :], eq[:, :, :],
                                           prio[:, :].rearrange("p (o q) -> p o q", o=1).broadcast_to((P, CT, PATHS)),
                                           ALU.mult), at)
                    link(dve.tensor_reduce(best[:, 1, :], sc[:, :, :], AX_X, ALU.max), at)
                    dve.tensor_tensor(pick[:, :, :], sc[:, :, :],
                                      best[:, 1, :].rearrange("p (t o) -> p t o", o=1).broadcast_to((P, CT, PATHS)),
                                      ALU.is_equal).then_inc(picked, 1)

                def turn(b, e, last):
                    total = TOTAL if not last else None
                    at = (A0 + TOTAL * b, total)
                    links[0] = 0
                    for c in range(CHUNKS):
                        n = CHUNKS * b + c
                        choose(n, at)
                        dve.wait_ge(o_made, 2 * n)
                        for i, m in enumerate(list(range(LAST)) + [LAST]):
                            rows = P if m < LAST else DM
                            dve.wait_ge(k_made, MC * n + i + 1)
                            dve.wait_ge(h_kept, (MC + 1) * (n + 1))
                            dve.tensor_tensor(hm[0:rows, m, :], ps_k[0:rows, :], hid[0:rows, m, :], ALU.mult)\
                               .then_inc(hm_done, 1)
                        if not last:
                            if c == 0:
                                layernorm(b + 1, 1 - e, at)
                                normalize(b + 1, 1 - e, 5 * b + 2)
                            else:
                                mix(b + 1, 1 - e, at)
                        base = 5 * b + (2 if not last else 1) + 2 * c
                        tiles = slice(c * CT, (c + 1) * CT)
                        for r in range(2):
                            dve.wait_ge(o_made, 2 * n + r + 1)
                            dve.tensor_tensor(y[:, 2 * r:2 * r + 2, :], ps_o[:, r, :, :],
                                              x1[:, e, c * CT + 2 * r:c * CT + 2 * r + 2, :], ALU.add)\
                               .then_inc(y_done, 1)
                        dve.wait_ge(y_done, 2 * n + 2)
                        dve.sem_inc(carrier, 1)
                        statistics(y, CT, st_b, mv_b, ve_b[:, :], at)
                        dve.wait_ge(rs_done, base + 1)
                        for i in range(CT):
                            ins = dve.tensor_scalar(z[:, i, :], y[:, i, :], mv_b[:, i, 0:1], rs_b[:, 0, i:i + 1],
                                                    ALU.subtract, ALU.mult)
                        link(ins, at)
                        link(dve.tensor_tensor(y[:, :, :], z[:, :, :],
                                               gb[:, 0, :].rearrange("p (o d) -> p o d", o=1).broadcast_to((P, CT, D)),
                                               ALU.mult), at)
                        dve.wait_ge(xb_done, n + 1)
                        link(dve.tensor_tensor(z[:, :, :], y[:, :, :], xb[:, :, :], ALU.add), at)
                        dve.sem_inc(carrier, 1)
                        statistics(z, CT, st_b, mv_b, ve_b[:, :], at)
                        dve.wait_ge(stored, 16 * CHUNKS * b)
                        dve.wait_ge(rs_done, base + 2)
                        for i in range(CT):
                            ins = dve.tensor_scalar(res[:, c, i, :], z[:, i, :], mv_b[:, i, 0:1],
                                                    rs_b[:, 1, i:i + 1], ALU.subtract, ALU.mult)
                        ins.then_inc(res_done, 1)
                    assert last or links[0] == TOTAL, links

                A0, TOTAL = 2 + 5, 2 * 5 + 2 + 5 + 2 * (2 + 3 + 2)
                layernorm(0, 0, (0, None))
                normalize(0, 0, 1)
                mix(0, 0, (0, None))
                assert links[0] == A0, links
                turns(dve, turn)

            @block.tensor
            def _(pe):
                pe.wait_ge(w_loaded, WL)
                pe.wait_ge(pool_const, 6 + KC + PATHS)
                WC = HEADS * HD // P
                for a in range(WC):
                    last_mm = pe.matmul(ps_o[:, 0, 0, :], ones[:, :], wout_sb[:, a, :],
                                        start=(a == 0), stop=(a == WC - 1))
                last_mm.then_inc(bcast_made, 1)
                for i in range(2):
                    pe.matmul(ps_h[:, i, 0:D], ones[0:1, :], row[:, i * D:(i + 1) * D], start=True, stop=True)\
                      .then_inc(bcast_made, 1)
                pe.matmul(ps_c[:, 0:PATHS], ones[0:1, :], row[:, 2 * D:2 * D + PATHS], start=True, stop=True)\
                  .then_inc(bcast_made, 1)
                pe.wait_ge(bcast_kept, 4)

                def stage_a(b, e):
                    pe.wait_ge(x1_done, b + 1)
                    for g in range(CHUNKS):
                        for k in range(KC):
                            pe.wait_ge(xt_kept, 4 * b + 2 * g if g else 4 * b)
                            for t in range(CT):
                                ins = pe.transpose(ps_t[:, k, t * P:(t + 1) * P],
                                                   x1[:, e, g * CT + t, k * P:(k + 1) * P], ident[:, :])
                            ins.then_inc(xt_made, 1)

                def turn(b, e, last):
                    pe.wait_ge(xm_done, b + 1)
                    for c in range(CHUNKS):
                        n = CHUNKS * b + c

                        def hidden(i):
                            m = LAST if i == 0 else i - 1
                            if i >= 1:
                                pe.wait_ge(h_kept, (MC + 1) * n + (0 if i == 1 else i))
                            else:
                                pe.wait_ge(h_kept, (MC + 1) * n)
                            for k in range(KC):
                                ins = pe.matmul(ps_h[:, i % 2, :],
                                                w1_sb[:, k, 2 * m:2 * m + 2, :].rearrange("d p m -> d (p m)"),
                                                xm[:, e, k, c * CHUNK:(c + 1) * CHUNK],
                                                start=(k == 0), stop=(k == KC - 1))
                            ins.then_inc(h_made, 1)

                        hidden(0)
                        hidden(1)
                        pe.wait_ge(h_kept, (MC + 1) * n + 1)
                        for t in range(CT):
                            ins = pe.matmul(ps_c[:, t * PATHS:(t + 1) * PATHS], hid[DM:P, LAST, t * P:(t + 1) * P],
                                            wo2_sb[DM:P, :], start=True, stop=True)
                        ins.then_inc(sc_made, 1)
                        for i in range(2, MC):
                            hidden(i)
                        pe.wait_ge(picked, n + 1)
                        for t in range(CT):
                            ins = pe.transpose(ps_pick[0:PATHS, t * P:(t + 1) * P], pick[:, t, :], ident16[:, :])
                        ins.then_inc(pick_made, 1)
                        pe.wait_ge(pick_kept, 2 * n + 1)
                        for i in range(MC):
                            pe.wait_ge(hm_done, MC * n + i)
                            pe.matmul(ps_k[:, :], widen[:, 2 * i:2 * i + 2, :].rearrange("p q m -> p (q m)"),
                                      pick_t[:, :], start=True, stop=True).then_inc(k_made, 1)
                        pe.wait_ge(hm_done, MC * (n + 1))
                        pe.wait_ge(pick_kept, 2 * n + 2)
                        for t in range(CT):
                            if t % 2 == 0:
                                pe.wait_ge(y_done, 2 * n)
                            for m in range(MC):
                                rows = P if m < LAST else X2
                                ins = pe.matmul(ps_o[:, t // 2, t % 2, :], hm[0:rows, m, t * P:(t + 1) * P],
                                                w2_sb[0:rows, m, :], start=(m == 0), stop=(m == LAST))
                            if t % 2:
                                ins.then_inc(o_made, 1)
                        if c == 0 and not last:
                            stage_a(b + 1, 1 - e)

                stage_a(0, 0)
                turns(pe, turn)


_INS = ['L0_attn_x', 'L0_attn_W_qkv', 'L0_attn_W_out', 'L0_ffn_mix_kernel', 'L0_ffn_W1', 'L0_ffn_b1',
        'L0_ffn_W2', 'L0_ffn_b2', 'L0_ffn_Wo1', 'L0_ffn_bo1', 'L0_ffn_Wo2', 'L0_ffn_bo2',
        'L0_ffn_gamma', 'L0_ffn_beta']


def layer(nc, x, w_qkv, w_out, mix_kernel, w1, b1, w2, b2, wo1, bo1, wo2, bo2, gamma, beta, out):
    qk_parts = nc.dram_tensor("qk_parts", (BATCH, 2 * HEADS * HD, PARTS, SEQ), BF16).ap()
    v_rows = nc.dram_tensor("v_rows", (BATCH, TILES, P, HEADS * VW), F32).ap()
    heads_out = nc.dram_tensor("heads_out", (BATCH, SEQ, D), F32).ap()
    project(nc, x, w_qkv, qk_parts, v_rows)
    attend(nc, qk_parts, v_rows, heads_out)
    feed(nc, x, heads_out, w_out, mix_kernel, w1, b1, w2, b2, wo1, bo1, wo2, bo2, gamma, beta, out)


def kernel(**inputs):
    import numpy as _np
    import concourse.bacc as _bacc
    from concourse import mybir as _mybir
    from concourse.bass_utils import run_bass_kernel_spmd as _run

    nc = _bacc.Bacc("TRN2", target_bir_lowering=False, num_devices=1)
    arrays, args = {}, []
    for name in _INS:
        a = _np.ascontiguousarray(inputs[name])
        arrays[f"in_{name}_dram"] = a
        args.append(nc.dram_tensor(f"in_{name}_dram", a.shape, _mybir.dt.from_np(a.dtype), kind="ExternalInput").ap())
    out = nc.dram_tensor("out_0_dram", (BATCH, SEQ, D), F32, kind="ExternalOutput").ap()
    layer(nc, *args, out)
    r = _run(nc, [arrays], core_ids=[0])
    return r.results[0]["out_0_dram"]
```

```python
from contextlib import ExitStack

import concourse.bass as bass
from concourse import mybir

ALU = mybir.AluOpType
ACT = mybir.ActivationFunctionType
AX_X = mybir.AxisListType.X
F32 = mybir.dt.float32
BF16 = mybir.dt.bfloat16

P = 128
BATCH, SEQ, D = 8, 1024, 256
HEADS, HD = 16, 16
KC = D // P
TILES = SEQ // P
CHUNK = 512
CHUNKS = SEQ // CHUNK
CT = CHUNK // P
QUAD = 4
QUADS = HEADS // QUAD
SLOTS = BATCH * QUADS
PARTS = 3
TERMS = [(0, 0), (0, 1), (0, 2), (1, 0), (1, 1), (2, 0)]
TROWS = len(TERMS) * HD
MROWS = TROWS + PARTS
SCALE = 0.25
NEG = -4.0e10
LOWEST = -3.0e38
VW = 2 * HD


def identity(eng, tile, done):
    eng.memset(tile[:, :], 0.0).then_inc(done, 1)
    eng.wait_ge(done, 1)
    eng.affine_select(out=tile[:, :], in_=tile[:, :], compare_op=ALU.not_equal, fill=1.0,
                      base=0, pattern=[[-1, P]], channel_multiplier=1).then_inc(done, 1)


def load_quad(sp, quads, qk_parts, v_rows, b, j):
    qs, ks, vq, loaded = quads
    for i, (pq, pk) in enumerate(TERMS):
        for dst, first, part in ((qs, 0, pq), (ks, HEADS * HD, pk)):
            r = first + j * QUAD * HD
            sp.dma_start(dst[i * HD:(i + 1) * HD, j, :, :],
                         qk_parts[b, r:r + QUAD * HD, part, :].rearrange("(n h) s -> h n s", h=HD))\
                .then_inc(loaded[j], 16)
    sp.dma_start(vq[:, j, :, :, :].rearrange("p t n v -> p t (n v)"),
                 v_rows[b, :, :, j * QUAD * VW:(j + 1) * QUAD * VW].rearrange("t p v -> p t v"))\
        .then_inc(loaded[j], 16)


def project(nc, x, w_qkv, qk_parts, v_rows, consts, quads):
    with ExitStack() as ctx:
        def sb(name, shape, dt):
            return ctx.enter_context(nc.sbuf_tensor(name, shape, dt))

        def pb(name, shape, dt):
            return ctx.enter_context(nc.psum_tensor(name, shape, dt))

        def sem(name):
            return ctx.enter_context(nc.semaphore(name))

        ident, ident16, mask16 = consts
        ks = quads[1]
        QKM = 2 * HEADS * HD // P
        HPC = P // HD
        w = sb("p_w", [P, KC, HEADS, 3 * HD], F32)
        wqk = sb("p_wqk", [P, KC, QKM, P], F32)
        wv = sb("p_wv", [P, KC, D], F32)
        x_rows = sb("p_x_rows", [P, CHUNKS, CT, D], F32)
        x_t = sb("p_x_t", [P, CHUNKS, KC, CHUNK], F32)
        parts = sb("p_parts", [P, CHUNKS, QKM, PARTS, CHUNK], BF16)
        rest = sb("p_rest", [P, QKM, CHUNK], F32)
        v_sb = sb("p_v_sb", [P, CHUNKS, CT, HEADS, VW], F32)
        ps_t = pb("p_ps_t", [P, KC, CHUNK], F32)
        ps_qk = pb("p_ps_qk", [P, QKM, CHUNK], F32)
        ps_v = pb("p_ps_v", [P, 2, 2, D], F32)

        w_loaded = sem("p_w_loaded")
        w_packed = sem("p_w_packed")
        ident_done = sem("p_ident_done")
        const_done = sem("p_const_done")
        ones_done = sem("p_ones_done")
        x_loaded = [sem(f"p_x_loaded{c}") for c in range(CHUNKS)]
        xt_made = sem("p_xt_made")
        xt_kept = sem("p_xt_kept")
        qk_made = sem("p_qk_made")
        v_made = sem("p_v_made")
        hi_done = sem("p_hi_done")
        rest_done = sem("p_rest_done")
        mid_done = sem("p_mid_done")
        lo_done = sem("p_lo_done")
        v_kept = sem("p_v_kept")
        parts_stored = [sem(f"p_parts_stored{c}") for c in range(CHUNKS)]
        v_stored = [sem(f"p_v_stored{c}") for c in range(CHUNKS)]

        with nc.Block() as block:
            @block.sync
            def _(sp):
                for c in range(KC):
                    sp.dma_start(w[:, c, :, :], w_qkv[:, c * P:(c + 1) * P, :].rearrange("n p e -> p n e"))\
                        .then_inc(w_loaded, 16)

                def load_x(b, c):
                    sp.dma_start(x_rows[:, c, :, :],
                                 x[b].rearrange("(t p) d -> p t d", p=P)[:, c * CT:(c + 1) * CT, :])\
                        .then_inc(x_loaded[c], 16)

                def store(b, c):
                    u = b * CHUNKS + c
                    for m in range(QKM):
                        sp.wait_ge(lo_done, u * QKM + m + 1)
                        sp.dma_start(qk_parts[b, m * P:(m + 1) * P, :, c * CHUNK:(c + 1) * CHUNK],
                                     parts[:, c, m, :, :]).then_inc(parts_stored[c], 16)
                    sp.wait_ge(v_kept, 2 * u + 2)
                    sp.dma_start(v_rows[b].rearrange("t p v -> p t v")[:, c * CT:(c + 1) * CT, :],
                                 v_sb[:, c, :, :, :].rearrange("p t n v -> p t (n v)"))\
                        .then_inc(v_stored[c], 16)

                def turn(b, last):
                    for c in range(CHUNKS):
                        if not last:
                            sp.wait_ge(xt_made, b * CHUNKS + c + 1)
                            load_x(b + 1, c)
                        store(b, c)

                for c in range(CHUNKS):
                    load_x(0, c)
                turn(0, False)
                turn(1, False)
                for c in range(CHUNKS):
                    sp.wait_ge(parts_stored[c], 16 * QKM)
                    sp.wait_ge(v_stored[c], 16)
                for j in range(2):
                    load_quad(sp, quads, qk_parts, v_rows, 0, j)
                    turn(2 + j, False)
                with sp.Fori(4, BATCH - 1) as b:
                    turn(b, False)
                turn(BATCH - 1, True)
                for c in range(CHUNKS):
                    sp.wait_ge(parts_stored[c], 16 * QKM * BATCH)
                    sp.wait_ge(v_stored[c], 16 * BATCH)

            @block.gpsimd
            def _(pool):
                identity(pool, ident, ident_done)
                pool.memset(mask16[:, :], 0.0).then_inc(const_done, 1)
                for j in range(QUADS):
                    pool.wait_ge(const_done, 1 + j)
                    pool.memset(ks[TROWS:P, j, :, :], 1.0).then_inc(const_done, 1)
                pool.wait_ge(const_done, 1 + QUADS)
                pool.affine_select(out=mask16[:, :], in_=mask16[:, :], compare_op=ALU.is_ge, fill=NEG,
                                   base=0, pattern=[[-1, P]], channel_multiplier=1).then_inc(const_done, 1)
                pool.wait_ge(ident_done, 2)
                pool.tensor_copy(ident16[:, :], ident[:, :]).then_inc(const_done, 1)

                def turn(b):
                    for c in range(CHUNKS):
                        u = b * CHUNKS + c
                        pool.wait_ge(parts_stored[c], 16 * QKM * b)
                        for m in range(QKM):
                            pool.wait_ge(mid_done, u * QKM + m + 1)
                            pool.tensor_tensor(parts[:, c, m, 2, :], rest[:, m, :], parts[:, c, m, 1, :],
                                               ALU.subtract).then_inc(lo_done, 1)

                turn(0)
                with pool.Fori(1, BATCH) as b:
                    turn(b)

            @block.vector
            def _(dve):
                dve.memset(v_sb[:, :, :, :, :].rearrange("p c t n v -> p (c t n) v")[:, :, HD:VW], 1.0)\
                   .then_inc(ones_done, 1)
                dve.wait_ge(w_loaded, 16 * KC)
                for qk in range(2):
                    for c in range(KC):
                        dve.tensor_copy(
                            wqk[:, c, qk * QKM // 2:(qk + 1) * QKM // 2, :]
                            .rearrange("p m (n h) -> p (m n) h", h=HD),
                            w[:, c, :, qk * HD:(qk + 1) * HD]).then_inc(w_packed, 1)
                for c in range(KC):
                    dve.tensor_copy(wv[:, c, :].rearrange("p (n h) -> p n h", h=HD),
                                    w[:, c, :, 2 * HD:3 * HD]).then_inc(w_packed, 1)
                def turn(b):
                    for c in range(CHUNKS):
                        u = b * CHUNKS + c
                        dve.wait_ge(lo_done, u * QKM)
                        for m in range(QKM):
                            dve.wait_ge(hi_done, u * QKM + m + 1)
                            dve.tensor_tensor(rest[:, m, :], ps_qk[:, m, :], parts[:, c, m, 0, :],
                                              ALU.subtract).then_inc(rest_done, 1)

                turn(0)
                with dve.Fori(1, BATCH) as b:
                    turn(b)

            @block.scalar
            def _(act):
                act.wait_ge(ones_done, 1)

                def keep_x(b, c):
                    act.wait_ge(xt_made, b * CHUNKS + c + 1)
                    act.activation(x_t[:, c, :, :], ps_t[:, :, :], ACT.Copy).then_inc(xt_kept, 1)

                def turn(b, last):
                    for c in range(CHUNKS):
                        u = b * CHUNKS + c
                        if c + 1 < CHUNKS:
                            keep_x(b, c + 1)
                        elif not last:
                            keep_x(b + 1, 0)
                        act.wait_ge(parts_stored[c], 16 * QKM * b)
                        act.wait_ge(v_stored[c], 16 * b)
                        for m in range(QKM):
                            act.wait_ge(qk_made, u * QKM + m + 1)
                            act.activation(parts[:, c, m, 0, :], ps_qk[:, m, :], ACT.Copy)\
                               .then_inc(hi_done, 1)
                            act.wait_ge(rest_done, u * QKM + m + 1)
                            act.activation(parts[:, c, m, 1, :], rest[:, m, :], ACT.Copy)\
                               .then_inc(mid_done, 1)
                        for r in range(2):
                            act.wait_ge(v_made, 2 * u + r + 1)
                            act.activation(v_sb[:, c, 2 * r:2 * r + 2, :, 0:HD],
                                           ps_v[:, r, :, :].rearrange("p t (n h) -> p t n h", h=HD),
                                           ACT.Copy).then_inc(v_kept, 1)

                keep_x(0, 0)
                turn(0, False)
                with act.Fori(1, BATCH - 1) as b:
                    turn(b, False)
                turn(BATCH - 1, True)

            @block.tensor
            def _(pe):
                pe.wait_ge(ident_done, 2)
                pe.wait_ge(w_packed, 3 * KC)

                def transposes(b, c):
                    pe.wait_ge(x_loaded[c], 16 * b + 16)
                    pe.wait_ge(xt_kept, b * CHUNKS + c)
                    for k in range(KC):
                        for t in range(CT):
                            ins = pe.transpose(ps_t[:, k, t * P:(t + 1) * P],
                                               x_rows[:, c, t, k * P:(k + 1) * P], ident[:, :])
                    ins.then_inc(xt_made, 1)

                def turn(b, end):
                    for c in range(CHUNKS):
                        u = b * CHUNKS + c
                        if c + 1 < CHUNKS:
                            transposes(b, c + 1)
                        elif not end:
                            transposes(b + 1, 0)
                        pe.wait_ge(xt_kept, u + 1)
                        for m in range(QKM):
                            if not isinstance(u, int) or u:
                                pe.wait_ge(rest_done, (u - 1) * QKM + m + 1)
                            for k in range(KC):
                                last = pe.matmul(ps_qk[:, m, :], wqk[:, k, m, :], x_t[:, c, k, :],
                                                 start=(k == 0), stop=(k == KC - 1))
                            last.then_inc(qk_made, 1)
                        pe.wait_ge(v_kept, 2 * u)
                        for r in range(2):
                            for t in range(2):
                                for k in range(KC):
                                    s = (2 * r + t) * P
                                    last = pe.matmul(ps_v[:, r, t, :], x_t[:, c, k, s:s + P], wv[:, k, :],
                                                     start=(k == 0), stop=(k == KC - 1))
                            last.then_inc(v_made, 1)

                transposes(0, 0)
                turn(0, False)
                with pe.Fori(1, BATCH - 1) as b:
                    turn(b, False)
                turn(BATCH - 1, True)


class Division:

    def __init__(self, nc, ctx, inv_rows, heads_out):
        def sb(name, shape):
            return ctx.enter_context(nc.sbuf_tensor(name, shape, F32))

        def sem(name):
            return ctx.enter_context(nc.semaphore(name))

        self.inv_rows, self.heads_out = inv_rows, heads_out
        self.o_sb = sb("a_o_sb", [P, 2, CHUNKS, CHUNK])
        self.sums = sb("a_sums", [P, QUAD * SEQ // P])
        self.inv = sb("a_inv", [P, QUAD * SEQ // P])
        self.wide = sb("a_wide", [P, CHUNKS, CHUNK])
        self.out_sb = sb("a_out_sb", [P, 2, 64, SEQ // 64])
        self.o_kept = sem("a_o_kept")
        self.sums_spread = sem("a_sums_spread")
        self.inv_done = sem("a_inv_done")
        self.inv_stored = sem("a_inv_stored")
        self.wide_loaded = sem("a_wide_loaded")
        self.out_done = sem("a_out_done")
        self.out_sent = [sem(f"a_out_sent{e}") for e in range(2)]

    def spread_divisors(self, sp, t, e):
        sp.wait_ge(self.o_kept, CHUNKS * (t + 1))
        sp.dma_start(self.sums[:, :],
                     self.o_sb[HD:P:VW, e, :, :].rearrange("n c (i q) -> n (c i) q", q=QUAD * SEQ // P))\
            .then_inc(self.sums_spread, 16)
        sp.wait_ge(self.inv_done, t + 1)
        sp.dma_start(self.inv_rows.rearrange("n (i q) -> (n i) q", q=QUAD * SEQ // P), self.inv[:, :])\
            .then_inc(self.inv_stored, 16)
        sp.wait_ge(self.inv_stored, 16 * (t + 1))
        sp.dma_start(self.wide[:, :, :].rearrange("p c q -> p (c q)"),
                     self.inv_rows.rearrange("n (o q) -> n o q", o=1).broadcast_to((QUAD, VW, SEQ)))\
            .then_inc(self.wide_loaded, 16)

    def send_out(self, sp, b, j):
        sp.wait_ge(self.out_done, CHUNKS * (QUADS * b + j + 1))
        for n in range(QUAD):
            dst = self.heads_out[b].rearrange("(r h) (n i) -> n h r i", h=HD, i=SEQ // 64)
            sp.dma_start(dst[j * QUAD + n], self.out_sb[n * VW:n * VW + HD, j % 2, :, :])\
                .then_inc(self.out_sent[j % 2], 16)

    def invert(self, dve, t):
        dve.wait_ge(self.sums_spread, 16 * (t + 1))
        dve.reciprocal(self.inv[:, :], self.sums[:, :]).then_inc(self.inv_done, 1)

    def form_out(self, dve, b, j, c):
        t, e = QUADS * b + j, j % 2
        dve.wait_ge(self.wide_loaded, 16 * (t + 1))
        dve.wait_ge(self.out_sent[e], 16 * QUAD * (QUADS // 2 * b + j // 2))
        dve.tensor_tensor(self.out_sb[:, e, :, 8 * c:8 * c + 8].rearrange("p r i -> p i r"),
                          self.wide[:, c, :].rearrange("p (i r) -> p i r", r=64),
                          self.o_sb[:, e, c, :].rearrange("p (i r) -> p i r", r=64), ALU.mult)\
           .then_inc(self.out_done, 1)


def attend(nc, qk_parts, v_rows, division, consts, quads, load_weights, load_in):
    with ExitStack() as ctx:
        def sb(name, shape, dt):
            return ctx.enter_context(nc.sbuf_tensor(name, shape, dt))

        def pb(name, shape, dt):
            return ctx.enter_context(nc.psum_tensor(name, shape, dt))

        def sem(name):
            return ctx.enter_context(nc.semaphore(name))

        ident, ident16, mask16 = consts
        qs, ks, vq, loaded = quads
        o_sb, o_kept, out_done = division.o_sb, division.o_kept, division.out_done
        STEPS = [(c, kt) for c in range(CHUNKS) for kt in range(CT * (c + 1))]
        NST = len(STEPS)
        PIECES = [(h, qt, s, min((qt + 1) * P - s, CHUNK), s // CHUNK)
                  for h in range(QUAD) for qt in range(TILES) for s in range(0, (qt + 1) * P, CHUNK)]
        NPC = len(PIECES)
        WIDTHS = [160 + min(CHUNK, (c + 1) * CHUNK - kt * P) for c, kt in STEPS]
        ENDS = []
        for st in range(NST):
            due = sum(p[3] for p in PIECES) * sum(WIDTHS[:st + 1]) // sum(WIDTHS)
            ENDS.append(sum(sum(p[3] for p in PIECES[:i + 1]) <= due for i in range(NPC)))
        SHARE = [range(a, b) for a, b in zip([0] + ENDS, ENDS)]
        PB = 3
        BANKS = 3
        RBANKS = 4
        assert NPC % RBANKS == 0 and QUAD * NST % BANKS == 0
        LOADS = 16 * (2 * len(TERMS) + 1)

        probs = sb("a_probs", [P, PB, QUAD, CHUNK], F32)
        mx = sb("a_mx", [P, 2, 2, QUAD, TILES], F32)
        mask_row = sb("a_mask_row", [P, CHUNK], F32)
        unused = sb("a_unused", [P, 2, CHUNK], F32)
        mrow = sb("a_mrow", [QUAD * TILES, PARTS, P], BF16)
        mrest = sb("a_mrest", [QUAD * TILES, P], F32)
        ps_s = pb("a_ps_s", [P, BANKS, CHUNK], F32)
        ps_m = pb("a_ps_m", [P, RBANKS, CHUNK], F32)
        ps_o = pb("a_ps_o", [P, CHUNK], F32)
        TURN = 2 * RBANKS + 1
        ps_x = ps_m[0:QUAD * TILES, TURN % RBANKS, 0:P]

        mask_made = sem("a_mask_made")
        carrier = sem("a_carrier")
        rows_made = sem("a_rows_made")
        rows_max = sem("a_rows_max")
        max_done = sem("a_max_done")
        max_t = sem("a_max_t")
        max_split = sem("a_max_split")
        max_sent = sem("a_max_sent")
        scores = sem("a_scores")
        exps = [sem(f"a_exps{e}") for e in range(2)]
        mask_turn = sem("a_mask_turn")
        masked = sem("a_masked")
        pv_done = sem("a_pv_done")

        def on_vector(i):
            h, qt, s, width, half = PIECES[i]
            return s + width == (qt + 1) * P and qt % 2 == 1

        VECTOR = [i for i in range(NPC) if on_vector(i)]

        def part(share, g):
            n = len(share)
            at = sorted(([2, 4, 2, 4, 1, 4] + n * [4])[:n])
            return [i for i, a in zip(share, at) if a == g]

        def step_shape(st):
            c, kt = STEPS[st]
            off = max(kt * P - c * CHUNK, 0)
            return off, CHUNK - off

        with nc.Block() as block:
            @block.sync
            def _(sp):
                def send_max(t, j):
                    sp.wait_ge(max_split, 4 * t + 4)
                    for i in range(PARTS):
                        sp.dma_start(qs[TROWS + i:TROWS + i + 1, j, :, :]
                                     .rearrange("o n (t q) -> o (n t) q", q=P),
                                     mrow[:, i, :]).then_inc(max_sent, 16)

                def turn(b, last):
                    for j in range(QUADS):
                        t = QUADS * b + j
                        if not (last and j == QUADS - 1):
                            send_max(t + 1, (j + 1) % QUADS)
                        if not (isinstance(t, int) and t == 0):
                            before, jb = (b, j - 1) if j else (b - 1, QUADS - 1)
                            division.spread_divisors(sp, t - 1, (j - 1) % 2)
                            if not (last and j):
                                sp.wait_ge(pv_done, NST * t)
                                load_quad(sp, quads, qk_parts, v_rows, before + 1, jb)
                            division.send_out(sp, before, jb)

                for j in range(2, QUADS):
                    load_quad(sp, quads, qk_parts, v_rows, 0, j)
                send_max(0, 0)
                turn(0, False)
                load_weights(sp)
                with sp.Fori(1, BATCH - 1) as b:
                    turn(b, False)
                for e in range(2):
                    sp.wait_ge(division.out_sent[e], 16 * QUAD * QUADS // 2)
                load_in(sp, 0)
                turn(BATCH - 1, True)

            @block.gpsimd
            def _(pool):
                def turn(b):
                    for j in range(QUADS):
                        t = QUADS * b + j
                        for st, (c, kt) in enumerate(STEPS):
                            if kt < c * CT:
                                continue
                            pool.wait_ge(exps[1], 2 * (NST * t + st + 1))
                            pool.sem_inc(mask_turn, 1)
                            tile = probs[:, st % PB, :, 0:P]
                            pool.affine_select(out=tile, in_=tile, compare_op=ALU.is_ge, fill=0.0, base=0,
                                               pattern=[[0, QUAD], [1, P]], channel_multiplier=-1)\
                                .then_inc(masked, 1)

                turn(0)
                with pool.Fori(1, BATCH) as b:
                    turn(b)

            @block.scalar
            def _(act):
                def keep_o(t, e, c):
                    act.wait_ge(pv_done, NST * t + (CT if c == 0 else NST))
                    if not (isinstance(t, int) and t < 2):
                        act.wait_ge(out_done, CHUNKS * (t - 1))
                    act.activation(o_sb[:, e, c, :], ps_o[:, :], ACT.Copy).then_inc(o_kept, 1)

                def turn(b):
                    for j in range(QUADS):
                        t = QUADS * b + j
                        for st, (c, kt) in enumerate(STEPS):
                            off, width = step_shape(st)
                            if st >= PB or not (isinstance(t, int) and t == 0):
                                act.wait_ge(pv_done, NST * t + st - PB + 1)
                            for h in range(QUAD):
                                n = QUAD * st + h
                                act.wait_ge(scores, QUAD * NST * t + n + 1)
                                act.activation(probs[:, st % PB, h, 0:width], ps_s[:, n % BANKS, 0:width],
                                               ACT.Exp, scale=SCALE).then_inc(exps[h % 2], 1)
                            if st == 0 and not (isinstance(t, int) and t == 0):
                                keep_o(t - 1, (j - 1) % 2, 1)
                            if st == CT:
                                keep_o(t, j % 2, 0)

                turn(0)
                with act.Fori(1, BATCH) as b:
                    turn(b)
                keep_o(SLOTS - 1, (QUADS - 1) % 2, 1)

            @block.vector
            def _(dve):
                def take_max(v, e, i):
                    h, qt, s, width, half = PIECES[i]
                    dve.wait_ge(rows_made, NPC * v + i + 1)
                    if on_vector(i):
                        k = VECTOR.index(i)
                        if k >= 2:
                            dve.wait_ge(rows_max, NPC * v + VECTOR[k - 2] + 1)
                        elif not (isinstance(v, int) and v == 0):
                            dve.wait_ge(rows_max, NPC * (v - 1) + VECTOR[k - 2] + 1)
                        dve.sem_inc(carrier, 1)
                        dve.tensor_tensor_reduce(out=unused[:, k % 2, 0:width], in0=ps_m[:, i % RBANKS, 0:width],
                                                 in1=mask_row[:, CHUNK - width:CHUNK], scale=1.0, scalar=LOWEST,
                                                 op0=ALU.add, op1=ALU.max,
                                                 accum_out=mx[:, e, half, h, qt:qt + 1]).then_inc(rows_max, 1)
                    else:
                        dve.tensor_reduce(mx[:, e, half, h, qt:qt + 1], ps_m[:, i % RBANKS, 0:width],
                                          AX_X, ALU.max).then_inc(rows_max, 1)

                def join_max(v, e):
                    dve.wait_ge(rows_max, NPC * (v + 1))
                    dve.tensor_tensor(mx[:, e, 0, :, CT:TILES], mx[:, e, 0, :, CT:TILES],
                                      mx[:, e, 1, :, CT:TILES], ALU.max).then_inc(max_done, 1)

                def split_max(v):
                    dve.wait_ge(max_t, v + 1)
                    src = ps_x
                    dve.wait_ge(max_sent, 16 * PARTS * v)
                    dve.tensor_scalar(mrow[:, 0, :], src, -1.0, None, ALU.mult).then_inc(max_split, 1)
                    dve.wait_ge(max_split, 4 * v + 1)
                    dve.scalar_tensor_tensor(out=mrest[:, :], in0=src, scalar=-1.0, in1=mrow[:, 0, :],
                                             op0=ALU.mult, op1=ALU.subtract).then_inc(max_split, 1)
                    dve.wait_ge(max_split, 4 * v + 2)
                    dve.tensor_copy(mrow[:, 1, :], mrest[:, :]).then_inc(max_split, 1)
                    dve.wait_ge(max_split, 4 * v + 3)
                    dve.tensor_tensor(mrow[:, 2, :], mrest[:, :], mrow[:, 1, :], ALU.subtract)\
                       .then_inc(max_split, 1)

                dve.memset(mask_row[:, :], 0.0).then_inc(mask_made, 1)
                dve.wait_ge(mask_made, 1)
                dve.tensor_copy(mask_row[:, CHUNK - P:CHUNK], mask16[:, :]).then_inc(mask_made, 1)
                dve.wait_ge(mask_made, 2)
                for v in range(2):
                    if v:
                        join_max(0, 0)
                    for i in range(NPC):
                        if v and i == TURN - 2:
                            split_max(0)
                        take_max(v, v, i)

                FORM = (8, 10)

                def turn(b, last):
                    for j in range(QUADS):
                        t = QUADS * b + j
                        more = not (last and j + 2 >= QUADS)
                        after = not (last and j == QUADS - 1)
                        before = not (isinstance(t, int) and t == 0)
                        if after:
                            join_max(t + 1, (j + 1) % 2)
                        for st in range(NST):
                            if more:
                                for i in SHARE[st]:
                                    if i == TURN - 2:
                                        split_max(t + 1)
                                    take_max(t + 2, j % 2, i)
                            elif after and st == 0:
                                split_max(t + 1)
                            if before and st == 4:
                                division.invert(dve, t - 1)
                            if before and st in FORM:
                                division.form_out(dve, *((b, j - 1) if j else (b - 1, QUADS - 1)), FORM.index(st))

                turn(0, False)
                with dve.Fori(1, BATCH - 1) as b:
                    turn(b, False)
                turn(BATCH - 1, True)

            @block.tensor
            def _(pe):
                def rows(v, j, i):
                    h, qt, s, width, half = PIECES[i]
                    if i >= RBANKS or not (isinstance(v, int) and v == 0):
                        pe.wait_ge(rows_max, NPC * v + i - RBANKS + 1)
                        if i == TURN and not (isinstance(v, int) and v == 0):
                            pe.wait_ge(max_split, 4 * v - 2)
                    out = ps_m[:, i % RBANKS, :]
                    own = s + width == (qt + 1) * P and not on_vector(i)
                    last = pe.matmul(out[:, 0:width], qs[0:TROWS, j, h, qt * P:(qt + 1) * P],
                                     ks[0:TROWS, j, h, s:s + width], start=True, stop=not own)
                    if own:
                        last = pe.matmul(out[:, width - P:width], ident16[:, :], mask16[:, :],
                                         start=False, stop=True)
                    last.then_inc(rows_made, 1)

                def turn_max(v, e, more):
                    pe.wait_ge(max_done, v + 1)
                    if more:
                        pe.wait_ge(rows_max, NPC * (v + 1) + TURN - RBANKS + 1)
                    pe.transpose(ps_x, mx[:, e, 0, :, :].rearrange("p n t -> p (n t)"),
                                 ident[:, :]).then_inc(max_t, 1)

                for v in range(2):
                    pe.wait_ge(loaded[v], LOADS)
                    for i in range(NPC):
                        if v and i == TURN - 1:
                            turn_max(0, 0, True)
                        rows(v, v, i)

                def products(t, j, st):
                    c, kt = STEPS[st]
                    off, width = step_shape(st)
                    pe.wait_ge(exps[1], 2 * (NST * t + st + 1))
                    if kt >= c * CT:
                        own = sum(k >= cc * CT for cc, k in STEPS[:st + 1])
                        pe.wait_ge(masked, TILES * t + own)
                    if kt == 0:
                        pe.wait_ge(o_kept, CHUNKS * t + c)
                    for h in range(QUAD):
                        last = pe.matmul(ps_o[h * VW:(h + 1) * VW, off:CHUNK], vq[:, j, kt, h, :],
                                         probs[:, st % PB, h, 0:width],
                                         start=(kt == 0), stop=(kt == CT * (c + 1) - 1))
                    last.then_inc(pv_done, 1)

                def turn(b, last):
                    for j in range(QUADS):
                        t = QUADS * b + j
                        more = not (last and j + 2 >= QUADS)
                        after = not (last and j == QUADS - 1)
                        before = not (isinstance(t, int) and t == 0)
                        jm = (j + 2) % QUADS
                        pe.wait_ge(max_sent, 16 * PARTS * (t + 1))
                        if more:
                            pe.wait_ge(loaded[jm], LOADS * (b + 1 + (j + 2) // QUADS))
                        for st, (c, kt) in enumerate(STEPS):
                            off, width = step_shape(st)
                            q0 = c * CHUNK + off
                            for h in range(QUAD):
                                n = QUAD * st + h
                                if before or n >= BANKS:
                                    pe.wait_ge(exps[(n - BANKS) % 2], 2 * NST * t + (n - BANKS) // 2 + 1)
                                pe.matmul(ps_s[:, n % BANKS, 0:width], ks[0:MROWS, j, h, kt * P:(kt + 1) * P],
                                          qs[0:MROWS, j, h, q0:q0 + width], start=True, stop=True)\
                                  .then_inc(scores, 1)
                                if more:
                                    for i in part(SHARE[st], h):
                                        if i == TURN - 1:
                                            turn_max(t + 1, (j + 1) % 2, True)
                                        rows(t + 2, jm, i)
                            if st == 1 and after and not more:
                                turn_max(t + 1, (j + 1) % 2, False)
                            if st >= 1:
                                products(t, j, st - 1)
                            elif before:
                                products(t - 1, (j - 1) % QUADS, NST - 1)
                            if more:
                                for i in part(SHARE[st], QUAD):
                                    if i == TURN - 1:
                                        turn_max(t + 1, (j + 1) % 2, True)
                                    rows(t + 2, jm, i)
                turn(0, False)
                with pe.Fori(1, BATCH - 1) as b:
                    turn(b, False)
                turn(BATCH - 1, True)
                products(SLOTS - 1, QUADS - 1, NST - 1)


def feed(nc, division, inputs, load_in, weights, w_loaded, out):
    with ExitStack() as ctx:
        def sb(name, shape, dt):
            return ctx.enter_context(nc.sbuf_tensor(name, shape, dt))

        def pb(name, shape, dt):
            return ctx.enter_context(nc.psum_tensor(name, shape, dt))

        def sem(name):
            return ctx.enter_context(nc.semaphore(name))

        x_in, a_in, in_loaded = inputs
        w1_sb, w2_sb, wo2_sb, bias, mixk, wout_sb, row = weights
        PATHS, DM = w1_sb.shape[2] - 1, w1_sb.shape[3]
        MC = w2_sb.shape[1]
        LAST = MC - 1
        WEIGHT_DMAS = 16 * (4 + 3 * KC + 2 * LAST + 5)
        EPS = 1e-5
        X2 = DM + PATHS

        ones = sb("f_ones", [P, P], F32)
        wsum = sb("f_wsum", [P, D], F32)
        gb = sb("f_gb", [P, 2, D], F32)
        bo2_sb = sb("f_bo2", [P, PATHS], F32)
        prio = sb("f_prio", [P, PATHS], F32)
        ident = sb("f_ident", [P, P], F32)
        ident16 = sb("f_ident16", [P, P], BF16)
        widen = sb("f_widen", [P, PATHS + 1, DM], BF16)
        half = sb("f_half", [P, TILES], F32)

        aw = sb("f_aw", [P, TILES, D], F32)
        x1 = sb("f_x1", [P, 2, TILES, D], F32)
        x1_t = sb("f_x1_t", [P, KC, SEQ + 2], F32)
        xm = sb("f_xm", [P, 2, KC, SEQ], F32)
        mixa = sb("f_mixa", [P, KC, 2, SEQ], F32)
        st_a = sb("f_st_a", [P, TILES, 6], F32)
        mv_a = sb("f_mv_a", [P, TILES, 2], F32)
        ve_a = sb("f_ve_a", [P, TILES], F32)
        rs_a = sb("f_rs_a", [P, TILES], F32)
        nm_a = sb("f_nm_a", [P, TILES], F32)
        nb_a = sb("f_nb_a", [P, TILES], F32)

        hid = sb("f_hid", [P, MC, CHUNK], F32)
        hm = sb("f_hm", [P, 2, MC, CHUNK], F32)
        sc = sb("f_sc", [P, CT, PATHS], F32)
        eq = sb("f_eq", [P, CT, PATHS], F32)
        best = sb("f_best", [P, 2, CT], F32)
        pick = sb("f_pick", [P, CT, PATHS], BF16)
        pick_t = sb("f_pick_t", [P, CHUNK], BF16)
        y = sb("f_y", [P, CT, D], F32)
        z = sb("f_z", [P, CT, D], F32)
        xb = sb("f_xb", [P, CT, D], F32)
        st_b = sb("f_st_b", [P, CT, 6], F32)
        mv_b = sb("f_mv_b", [P, CT, 2], F32)
        ve_b = sb("f_ve_b", [P, CT], F32)
        rs_b = sb("f_rs_b", [P, 2, CT], F32)
        res = sb("f_res", [P, 2, CT, D], F32)

        ps_t = pb("f_ps_t", [P, 2, CHUNK], F32)
        ps_h = pb("f_ps_h", [P, 2, CHUNK], F32)
        ps_k = pb("f_ps_k", [P, CHUNK], F32)
        ps_o = pb("f_ps_o", [P, 2, 2, D], F32)
        ps_c = pb("f_ps_c", [P, CHUNK], F32)
        ps_pick = ps_c[:, CHUNK // 2:CHUNK].bitcast(BF16)

        mask_banks = [ps_h[:, 0, :], ps_h[:, 1, :], ps_k[:, :], ps_h[:, 1, :], ps_k[:, :]]

        const_done = sem("f_const_done")
        pool_const = sem("f_pool_const")
        ones_done = sem("f_ones_done")
        bcast_made = sem("f_bcast_made")
        bcast_kept = sem("f_bcast_kept")
        prod_done = sem("f_prod_done")
        aw_done = sem("f_aw_done")
        ve_done = sem("f_ve_done")
        rs_done = sem("f_rs_done")
        nb_done = sem("f_nb_done")
        x1_done = sem("f_x1_done")
        xt_made = sem("f_xt_made")
        xt_kept = sem("f_xt_kept")
        mix0_done = sem("f_mix0_done")
        xm_done = sem("f_xm_done")
        chain = sem("f_chain")
        h_made = sem("f_h_made")
        h_kept = sem("f_h_kept")
        sc_made = sem("f_sc_made")
        picked = sem("f_picked")
        pick_made = sem("f_pick_made")
        pick_kept = sem("f_pick_kept")
        k_made = sem("f_k_made")
        hm_done = sem("f_hm_done")
        o_made = sem("f_o_made")
        y_done = sem("f_y_done")
        xb_done = sem("f_xb_done")
        carrier = sem("f_carrier")
        res_done = sem("f_res_done")
        stored = sem("f_stored")

        def norms(b, c, last):
            if isinstance(b, int) and b == 0:
                return 2
            return 5 * b + 2 * c - (1 if last else 0)

        def turns(eng, turn):
            for e in range(2):
                turn(e, e, False)
            with eng.Fori(1, BATCH // 2 - 1) as pair:
                for e in range(2):
                    turn(2 * pair + e, e, False)
            for e in range(2):
                turn(BATCH - 2 + e, e, e == 1)

        with nc.Block() as block:
            @block.sync
            def _(sp):
                division.spread_divisors(sp, SLOTS - 1, 1)

                def store(b, c):
                    sp.wait_ge(res_done, CHUNKS * b + c + 1)
                    sp.dma_start(out[b].rearrange("(t p) d -> p t d", p=P)[:, c * CT:(c + 1) * CT, :],
                                 res[:, c, :, :]).then_inc(stored, 16)

                def turn(b, e, last):
                    if not isinstance(b, int) or b + 2 < BATCH:
                        sp.wait_ge(aw_done, b + 2)
                        load_in(sp, b + 2)
                    if not (isinstance(b, int) and b == 0):
                        store(b - 1, 1)
                    store(b, 0)
                    if isinstance(b, int) and b == 1:
                        for s in range(2):
                            sp.wait_ge(division.out_sent[s], 16 * QUAD * SLOTS // 2)

                sp.wait_ge(aw_done, 1)
                load_in(sp, 1)
                division.send_out(sp, BATCH - 1, QUADS - 1)
                turns(sp, turn)
                store(BATCH - 1, 1)
                sp.wait_ge(stored, 16 * CHUNKS * BATCH)

            @block.gpsimd
            def _(pool):
                pool.memset(ones[:, :], 1.0).then_inc(ones_done, 1)
                identity(pool, ident, const_done)
                pool.memset(widen[:, :, :], 0.0).then_inc(pool_const, 1)
                pool.memset(half[:, :], -0.5).then_inc(pool_const, 1)
                pool.memset(pick_t[:, :], 0.0).then_inc(pool_const, 1)
                for k in range(KC):
                    pool.memset(x1_t[:, k, 0:SEQ + 2:SEQ + 1], 0.0).then_inc(pool_const, 1)
                for p in range(PATHS):
                    pool.memset(prio[:, p:p + 1], float(PATHS - p)).then_inc(pool_const, 1)
                pool.wait_ge(const_done, 2)
                pool.tensor_copy(ident16[:, :], ident[:, :]).then_inc(pool_const, 1)
                pool.wait_ge(pool_const, 4 + KC + PATHS)
                pool.affine_select(out=widen[:, :, :], in_=widen[:, :, :], compare_op=ALU.not_equal, fill=1.0,
                                   base=0, pattern=[[-1, PATHS + 1], [0, DM]], channel_multiplier=1)\
                    .then_inc(pool_const, 1)
                pool.wait_ge(bcast_kept, 4)

                def rsqrt(count, ve, rs, k):
                    pool.wait_ge(ve_done, count)
                    pool.tensor_tensor(rs, ve, half[:, 0:k], ALU.pow).then_inc(rs_done, 1)

                def attention_sum(b):
                    pool.wait_ge(x1_done, CHUNKS * b)
                    pool.wait_ge(in_loaded, 32 * (b + 1))
                    pool.tensor_tensor(aw[:, :, :], a_in[:, :, :],
                                       wsum[:, :].rearrange("p (o d) -> p o d", o=1).broadcast_to((P, TILES, D)),
                                       ALU.mult).then_inc(prod_done, 1)
                    pool.wait_ge(prod_done, b + 1)
                    pool.tensor_tensor(aw[:, :, :], aw[:, :, :], x_in[:, :, :], ALU.add).then_inc(aw_done, 1)

                def scale_a(before):
                    rsqrt(before + 1, ve_a[:, :], rs_a[:, :], TILES)
                    pool.wait_ge(rs_done, before + 1)
                    pool.tensor_tensor(nb_a[:, :], nm_a[:, :], rs_a[:, :], ALU.mult).then_inc(nb_done, 1)

                def add_beta(n, e, c):
                    pool.wait_ge(res_done, n)
                    pool.tensor_tensor(xb[:, :, :], x1[:, e, c * CT:(c + 1) * CT, :],
                                       gb[:, 1, :].rearrange("p (o d) -> p o d", o=1).broadcast_to((P, CT, D)),
                                       ALU.add).then_inc(xb_done, 1)

                def finish(base):
                    for i in range(2):
                        rsqrt(base + i + 1, ve_b[:, :], rs_b[:, i, :], CT)

                def turn(b, e, last):
                    for c in range(CHUNKS):
                        before = c or not (isinstance(b, int) and b == 0)
                        if before:
                            add_beta(CHUNKS * b + c - 1, *((e, 0) if c else (1 - e, 1)))
                        if c == 0 and not last:
                            scale_a(norms(b, 0, last) - 1)
                        if c == 1 and (not isinstance(b, int) or b + 2 < BATCH):
                            attention_sum(b + 2)
                        if before:
                            finish(norms(b, c, last))

                scale_a(0)
                attention_sum(1)
                turns(pool, turn)
                add_beta(CHUNKS * BATCH - 1, 1, 1)
                finish(norms(BATCH, 0, True) - 1)

            @block.scalar
            def _(act):
                act.wait_ge(bcast_made, 1)
                act.activation(wsum[:, :], ps_o[:, 0, 0, :], ACT.Copy).then_inc(bcast_kept, 1)
                for i in range(2):
                    act.wait_ge(bcast_made, i + 2)
                    act.activation(gb[:, i, :], ps_h[:, i, 0:D], ACT.Copy).then_inc(bcast_kept, 1)
                act.wait_ge(bcast_made, 4)
                act.activation(bo2_sb[:, :], ps_c[:, 0:PATHS], ACT.Copy).then_inc(bcast_kept, 1)
                act.wait_ge(w_loaded, WEIGHT_DMAS)

                def normalize(b, e, used, g):
                    act.wait_ge(nb_done, b + 1)
                    act.wait_ge(xb_done, used)
                    act.wait_ge(y_done, 2 * used)
                    for i in range(g * CT, (g + 1) * CT):
                        ins = act.activation(x1[:, e, i, :], aw[:, i, :], ACT.Identity, scale=rs_a[:, i:i + 1],
                                             bias=nb_a[:, i:i + 1])
                    ins.then_inc(x1_done, 1)

                def keep_transposed(b, g):
                    act.wait_ge(xm_done, KC * b)
                    for k in range(KC):
                        act.wait_ge(xt_made, 4 * b + 2 * g + k + 1)
                        act.activation(x1_t[:, k, 1 + g * CHUNK:1 + (g + 1) * CHUNK], ps_t[:, k, :],
                                       ACT.Copy).then_inc(xt_kept, 1)

                def mix_first(b):
                    act.wait_ge(xt_kept, 4 * (b + 1))
                    for k in range(KC):
                        act.activation(mixa[:, k, 0, :], x1_t[:, k, 0:SEQ], ACT.Copy,
                                       scale=mixk[:, 0, k:k + 1]).then_inc(mix0_done, 1)

                def turn(b, e, last):
                    for c in range(CHUNKS):
                        n = CHUNKS * b + c
                        act.wait_ge(hm_done, MC * n)
                        act.wait_ge(h_made, MC * n + 1)
                        act.activation(hid[DM:P, LAST, :], ps_h[DM:P, 0, :], ACT.Tanh,
                                       bias=bias[DM:P, LAST:MC]).then_inc(h_kept, 1)
                        act.activation(hid[0:DM, LAST, :], ps_h[0:DM, 0, :], ACT.Identity,
                                       bias=bias[0:DM, LAST:MC]).then_inc(h_kept, 1)
                        for m in range(LAST):
                            act.wait_ge(h_made, MC * n + m + 2)
                            act.activation(hid[:, m, :], ps_h[:, (m + 1) % 2, :], ACT.Identity,
                                           bias=bias[:, m:m + 1]).then_inc(h_kept, 1)
                            if m < CHUNKS and c == 1 and not last:
                                normalize(b + 1, 1 - e, CHUNKS * b, m)
                        if c == 1 and not last:
                            for g in range(CHUNKS):
                                keep_transposed(b + 1, g)
                        act.wait_ge(pick_made, n + 1)
                        act.activation(pick_t[0:PATHS, :], ps_pick[0:PATHS, :], ACT.Copy).then_inc(pick_kept, 1)
                        if not (isinstance(n, int) and n < 2):
                            act.wait_ge(o_made, 2 * (n - 1))
                        act.activation(hm[DM:X2, c, LAST, :], ps_pick[0:PATHS, :], ACT.Copy).then_inc(pick_kept, 1)
                        if c == 1 and not last:
                            mix_first(b + 1)

                for g in range(CHUNKS):
                    normalize(0, 0, 0, g)
                for g in range(CHUNKS):
                    keep_transposed(0, g)
                mix_first(0)
                turns(act, turn)

            @block.vector
            def _(dve):
                dve.wait_ge(w_loaded, WEIGHT_DMAS)
                links = [0]

                def link(ins, turn):
                    base, total = turn
                    links[0] += 1
                    ins.then_inc(chain, 1)
                    dve.wait_ge(chain, base + links[0])

                def statistics(src, tiles, st, mv, ve, at, nm=None):
                    for i in range(tiles):
                        ins = dve.bn_stats(st[:, i, :], src[:, i, :])
                    link(ins, at)
                    dve.sem_inc(carrier, 1)
                    for i in range(tiles):
                        ins = dve.bn_aggr(mv[:, i, :], st[:, i, :])
                    link(ins, at)
                    if nm is not None:
                        dve.tensor_scalar(nm, mv[:, :, 0], -1.0, None, ALU.mult)
                    dve.tensor_scalar(ve, mv[:, :, 1], EPS, None, ALU.add).then_inc(ve_done, 1)

                def layernorm(b, at):
                    dve.wait_ge(aw_done, b + 1)
                    dve.sem_inc(carrier, 1)
                    statistics(aw, TILES, st_a, mv_a, ve_a[:, :], at, nm_a[:, :])

                def mix(b, e, k, at):
                    dve.wait_ge(mix0_done, KC * b + k + 1)
                    link(dve.scalar_tensor_tensor(out=mixa[:, k, 1, :], in0=x1_t[:, k, 1:SEQ + 1],
                                                  scalar=mixk[:, 1, k:k + 1], in1=mixa[:, k, 0, :],
                                                  op0=ALU.mult, op1=ALU.add), at)
                    dve.scalar_tensor_tensor(out=xm[:, e, k, :], in0=x1_t[:, k, 2:SEQ + 2],
                                             scalar=mixk[:, 2, k:k + 1], in1=mixa[:, k, 1, :],
                                             op0=ALU.mult, op1=ALU.add).then_inc(xm_done, 1)

                def choose(n, at):
                    dve.wait_ge(sc_made, n + 1)
                    link(dve.tensor_tensor(sc[:, :, :],
                                           ps_c[:, 0:CT * PATHS].rearrange("p (t q) -> p t q", q=PATHS),
                                           bo2_sb[:, :].rearrange("p (o q) -> p o q", o=1).broadcast_to((P, CT, PATHS)),
                                           ALU.add), at)
                    link(dve.tensor_reduce(best[:, 0, :], sc[:, :, :], AX_X, ALU.max), at)
                    link(dve.tensor_tensor(eq[:, :, :], sc[:, :, :],
                                           best[:, 0, :].rearrange("p (t o) -> p t o", o=1).broadcast_to((P, CT, PATHS)),
                                           ALU.is_equal), at)
                    link(dve.tensor_tensor(sc[:, :, :], eq[:, :, :],
                                           prio[:, :].rearrange("p (o q) -> p o q", o=1).broadcast_to((P, CT, PATHS)),
                                           ALU.mult), at)
                    link(dve.tensor_reduce(best[:, 1, :], sc[:, :, :], AX_X, ALU.max), at)
                    dve.tensor_tensor(pick[:, :, :], sc[:, :, :],
                                      best[:, 1, :].rearrange("p (t o) -> p t o", o=1).broadcast_to((P, CT, PATHS)),
                                      ALU.is_equal).then_inc(picked, 1)

                def keep_hidden(n, c, i):
                    rows = P if i < LAST else DM
                    dve.wait_ge(k_made, MC * n + i + 1)
                    dve.wait_ge(h_kept, (MC + 1) * (n + 1))
                    dve.tensor_tensor(hm[0:rows, c, i, :], mask_banks[i][0:rows, :], hid[0:rows, i, :], ALU.mult)\
                       .then_inc(hm_done, 1)

                def add_x1(n, e, c, r):
                    dve.wait_ge(o_made, 2 * n + r + 1)
                    dve.tensor_tensor(y[:, 2 * r:2 * r + 2, :], ps_o[:, r, :, :],
                                      x1[:, e, c * CT + 2 * r:c * CT + 2 * r + 2, :], ALU.add)\
                       .then_inc(y_done, 1)

                def finish(n, c, base, store_count, at):
                    dve.wait_ge(y_done, 2 * n + 2)
                    dve.sem_inc(carrier, 1)
                    statistics(y, CT, st_b, mv_b, ve_b[:, :], at)
                    for i in range(CT):
                        ins = dve.scalar_tensor_tensor(out=z[:, i, :], in0=y[:, i, :], scalar=mv_b[:, i, 0:1],
                                                       in1=gb[:, 0, :], op0=ALU.subtract, op1=ALU.mult)
                    link(ins, at)
                    dve.wait_ge(rs_done, base + 1)
                    dve.wait_ge(xb_done, n + 1)
                    for i in range(CT):
                        ins = dve.scalar_tensor_tensor(out=z[:, i, :], in0=z[:, i, :], scalar=rs_b[:, 0, i:i + 1],
                                                       in1=xb[:, i, :], op0=ALU.mult, op1=ALU.add)
                    link(ins, at)
                    dve.sem_inc(carrier, 1)
                    statistics(z, CT, st_b, mv_b, ve_b[:, :], at)
                    dve.wait_ge(stored, store_count)
                    dve.wait_ge(rs_done, base + 2)
                    for i in range(CT):
                        ins = dve.tensor_scalar(res[:, c, i, :], z[:, i, :], mv_b[:, i, 0:1],
                                                rs_b[:, 1, i:i + 1], ALU.subtract, ALU.mult)
                    ins.then_inc(res_done, 1)

                def turn(b, e, last):
                    first = isinstance(b, int) and b == 0
                    at = (A0 + (TOTAL * b - FINISH if not first else 0), None)
                    links[0] = 0
                    for c in range(CHUNKS):
                        n = CHUNKS * b + c
                        before = not (first and c == 0)
                        eb, cb = (e, 0) if c else (1 - e, 1)
                        choose(n, at)
                        if c == 0 and not last:
                            layernorm(b + 1, at)
                        if before:
                            add_x1(n - 1, eb, cb, 0)
                        for i in range(MC):
                            keep_hidden(n, c, i)
                            if i == 2 and c == 1 and not last:
                                for k in range(KC):
                                    mix(b + 1, 1 - e, k, at)
                        if before:
                            add_x1(n - 1, eb, cb, 1)
                        if before:
                            finish(n - 1, cb, norms(b, c, last), 16 * CHUNKS * (b if c else b - 1), at)
                    assert last or links[0] == TOTAL - (FINISH if first else 0), links

                FINISH = 2 + 2 + 2
                A0, TOTAL = 2 + KC, 2 * 5 + 2 + KC + 2 * FINISH
                dve.wait_ge(bcast_kept, 1)
                dve.wait_ge(in_loaded, 32)
                dve.tensor_tensor(aw[:, :, :], a_in[:, :, :],
                                  wsum[:, :].rearrange("p (o d) -> p o d", o=1).broadcast_to((P, TILES, D)),
                                  ALU.mult).then_inc(prod_done, 1)
                dve.wait_ge(prod_done, 1)
                dve.tensor_tensor(aw[:, :, :], aw[:, :, :], x_in[:, :, :], ALU.add).then_inc(aw_done, 1)
                division.invert(dve, SLOTS - 1)
                layernorm(0, (0, None))
                for c in range(CHUNKS):
                    division.form_out(dve, BATCH - 1, QUADS - 1, c)
                dve.wait_ge(bcast_kept, 4)
                for k in range(KC):
                    mix(0, 0, k, (0, None))
                assert links[0] == A0, links
                turns(dve, turn)
                for r in range(2):
                    add_x1(CHUNKS * BATCH - 1, 1, 1, r)
                finish(CHUNKS * BATCH - 1, 1, norms(BATCH, 0, True) - 1, 16 * CHUNKS * (BATCH - 1),
                       (A0 + TOTAL * (BATCH - 1) - FINISH, None))

            @block.tensor
            def _(pe):
                pe.wait_ge(w_loaded, WEIGHT_DMAS)
                pe.wait_ge(ones_done, 1)
                WC = HEADS * HD // P
                for a in range(WC):
                    last_mm = pe.matmul(ps_o[:, 0, 0, :], ones[:, :], wout_sb[:, a, :],
                                        start=(a == 0), stop=(a == WC - 1))
                last_mm.then_inc(bcast_made, 1)
                for i in range(2):
                    pe.matmul(ps_h[:, i, 0:D], ones[0:1, :], row[:, i * D:(i + 1) * D], start=True, stop=True)\
                      .then_inc(bcast_made, 1)
                pe.matmul(ps_c[:, 0:PATHS], ones[0:1, :], row[:, 2 * D:2 * D + PATHS], start=True, stop=True)\
                  .then_inc(bcast_made, 1)
                pe.wait_ge(bcast_kept, 4)
                pe.wait_ge(pool_const, 5 + KC + PATHS)

                def transposes(b, e, g, k):
                    pe.wait_ge(x1_done, CHUNKS * b + g + 1)
                    pe.wait_ge(xt_kept, 4 * b + 2 * g)
                    for t in range(CT):
                        ins = pe.transpose(ps_t[:, k, t * P:(t + 1) * P],
                                           x1[:, e, g * CT + t, k * P:(k + 1) * P], ident[:, :])
                    ins.then_inc(xt_made, 1)

                def output(n, c, t):
                    if t % 2 == 0:
                        pe.wait_ge(y_done, 2 * n)
                    for m in range(MC):
                        rows = P if m < LAST else X2
                        ins = pe.matmul(ps_o[:, t // 2, t % 2, :], hm[0:rows, c, m, t * P:(t + 1) * P],
                                        w2_sb[0:rows, m, :], start=(m == 0), stop=(m == LAST))
                    if t % 2:
                        ins.then_inc(o_made, 1)

                def turn(b, e, last):
                    pe.wait_ge(xm_done, KC * (b + 1))
                    for c in range(CHUNKS):
                        n = CHUNKS * b + c
                        before = not (isinstance(n, int) and n == 0)

                        def hidden(i):
                            m = LAST if i == 0 else i - 1
                            if i >= 2:
                                pe.wait_ge(h_kept, (MC + 1) * n + i)
                            if i < 2 and before:
                                pe.wait_ge(hm_done, MC * (n - 1) + (1, 4)[i])
                            for k in range(KC):
                                ins = pe.matmul(ps_h[:, i % 2, :],
                                                w1_sb[:, k, 2 * m:2 * m + 2, :].rearrange("d p m -> d (p m)"),
                                                xm[:, e, k, c * CHUNK:(c + 1) * CHUNK],
                                                start=(k == 0), stop=(k == KC - 1))
                            ins.then_inc(h_made, 1)

                        hidden(0)
                        hidden(1)
                        pe.wait_ge(h_kept, (MC + 1) * n + 1)
                        for t in range(CT):
                            ins = pe.matmul(ps_c[:, t * PATHS:(t + 1) * PATHS], hid[DM:P, LAST, t * P:(t + 1) * P],
                                            wo2_sb[DM:P, :], start=True, stop=True)
                        ins.then_inc(sc_made, 1)
                        for i in range(2, MC):
                            hidden(i)
                        before = not (isinstance(n, int) and n == 0)
                        if before:
                            pe.wait_ge(pick_kept, 2 * n)
                        for g in range(CHUNKS):
                            if c == 1 and not last:
                                for k in range(KC):
                                    transposes(b + 1, 1 - e, g, k)
                            if g == 0 and before:
                                output(n - 1, 1 - c, 0)
                        pe.wait_ge(picked, n + 1)
                        for t in range(CT):
                            ins = pe.transpose(ps_pick[0:PATHS, t * P:(t + 1) * P], pick[:, t, :], ident16[:, :])
                        ins.then_inc(pick_made, 1)
                        if before:
                            output(n - 1, 1 - c, 1)
                        pe.wait_ge(pick_kept, 2 * n + 1)
                        pe.wait_ge(h_kept, (MC + 1) * (n + 1))
                        for i in range(MC):
                            if i >= 3:
                                pe.wait_ge(hm_done, MC * n + i - 1)
                            pe.matmul(mask_banks[i], widen[:, 2 * i:2 * i + 2, :].rearrange("p q m -> p (q m)"),
                                      pick_t[:, :], start=True, stop=True).then_inc(k_made, 1)
                            if i in (2, 4) and before:
                                output(n - 1, 1 - c, 1 + i // 2)

                for g in range(CHUNKS):
                    for k in range(KC):
                        transposes(0, 0, g, k)
                turns(pe, turn)
                pe.wait_ge(hm_done, MC * CHUNKS * BATCH)
                pe.wait_ge(pick_kept, 2 * CHUNKS * BATCH)
                for t in range(CT):
                    output(CHUNKS * BATCH - 1, 1, t)


_INS = ['L0_attn_x', 'L0_attn_W_qkv', 'L0_attn_W_out', 'L0_ffn_mix_kernel', 'L0_ffn_W1', 'L0_ffn_b1',
        'L0_ffn_W2', 'L0_ffn_b2', 'L0_ffn_Wo1', 'L0_ffn_bo1', 'L0_ffn_Wo2', 'L0_ffn_bo2',
        'L0_ffn_gamma', 'L0_ffn_beta']


def layer(nc, x, w_qkv, w_out, mix_kernel, w1, b1, w2, b2, wo1, bo1, wo2, bo2, gamma, beta, out):
    qk_parts = nc.dram_tensor("qk_parts", (BATCH, 2 * HEADS * HD, PARTS, SEQ), BF16).ap()
    v_rows = nc.dram_tensor("v_rows", (BATCH, TILES, P, HEADS * VW), F32).ap()
    inv_rows = nc.dram_tensor("inv_rows", (QUAD, SEQ), F32).ap()
    heads_out = nc.dram_tensor("heads_out", (BATCH, SEQ, D), F32).ap()
    PATHS, _, DM = w1.shape
    MC = (PATHS + 1) * DM // P
    LAST = MC - 1
    X2 = DM + PATHS

    with ExitStack() as ctx:
        def sb(name, shape, dt, stack=ctx):
            return stack.enter_context(nc.sbuf_tensor(name, shape, dt))

        w1_sb = sb("f_w1", [P, KC, PATHS + 1, DM], F32)
        w2_sb = sb("f_w2", [P, MC, D], F32)
        wo2_sb = sb("f_wo2", [P, PATHS], F32)
        bias = sb("f_bias", [P, MC], F32)
        mixk = sb("f_mixk", [P, 3, KC], F32)
        wout_sb = sb("f_wout", [P, HEADS * HD // P, D], F32)
        row = sb("f_row", [1, 2 * D + PATHS], F32)
        x_in = sb("f_x_in", [P, TILES, D], F32)
        a_in = sb("f_a_in", [P, TILES, D], F32)
        w_loaded = ctx.enter_context(nc.semaphore("f_w_loaded"))
        in_loaded = ctx.enter_context(nc.semaphore("f_in_loaded"))

        def load_in(sp, b):
            sp.dma_start(x_in[:, :, :], x[b].rearrange("(t p) d -> p t d", p=P)).then_inc(in_loaded, 16)
            sp.dma_start(a_in[:, :, :], heads_out[b].rearrange("(t p) d -> p t d", p=P)).then_inc(in_loaded, 16)

        def load_weights(sp):
            sp.dma_start(wout_sb[:, :, :], w_out.rearrange("(a n) h d -> (n h) a d", n=P // HD))\
                .then_inc(w_loaded, 16)
            for i, v in enumerate((gamma, beta)):
                sp.dma_start(row[:, i * D:(i + 1) * D], v.rearrange("(a d) -> a d", a=1)).then_inc(w_loaded, 16)
            sp.dma_start(row[:, 2 * D:2 * D + PATHS], bo2.rearrange("(a d) -> a d", a=1)).then_inc(w_loaded, 16)
            for k in range(KC):
                rows = slice(k * P, (k + 1) * P)
                sp.dma_start(w1_sb[:, k, 0:PATHS, :], w1[:, rows, :].rearrange("p d m -> d p m"))\
                    .then_inc(w_loaded, 16)
                sp.dma_start(w1_sb[:, k, PATHS, :], wo1[rows, :]).then_inc(w_loaded, 16)
                sp.dma_start(mixk[:, :, k], mix_kernel[:, rows].rearrange("t d -> d t"),
                             allow_slow_non_contiguous=True).then_inc(w_loaded, 16)
            for m in range(LAST):
                sp.dma_start(w2_sb[:, m, :], w2[2 * m:2 * m + 2].rearrange("q m d -> (q m) d"))\
                    .then_inc(w_loaded, 16)
                sp.dma_start(bias[:, m:m + 1],
                             b1[2 * m:2 * m + 2].rearrange("q (m o) -> (q m) o", o=1)).then_inc(w_loaded, 16)
            sp.dma_start(w2_sb[0:DM, LAST, :], w2[PATHS - 1]).then_inc(w_loaded, 16)
            sp.dma_start(w2_sb[DM:X2, LAST, :], b2).then_inc(w_loaded, 16)
            sp.dma_start(bias[0:DM, LAST:MC], b1[PATHS - 1].rearrange("(m o) -> m o", o=1)).then_inc(w_loaded, 16)
            sp.dma_start(bias[DM:P, LAST:MC], bo1.rearrange("(m o) -> m o", o=1)).then_inc(w_loaded, 16)
            sp.dma_start(wo2_sb[DM:P, :], wo2).then_inc(w_loaded, 16)

        division = Division(nc, ctx, inv_rows, heads_out)
        with ExitStack() as inner:
            ident = sb("ident", [P, P], F32, inner)
            ident16 = sb("ident16", [P, P], BF16, inner)
            mask16 = sb("mask16", [P, P], BF16, inner)
            qs = sb("a_qs", [P, QUADS, QUAD, SEQ], BF16, inner)
            ks = sb("a_ks", [P, QUADS, QUAD, SEQ], BF16, inner)
            vq = sb("a_vq", [P, QUADS, TILES, QUAD, VW], F32, inner)
            loaded = [inner.enter_context(nc.semaphore(f"a_loaded{j}")) for j in range(QUADS)]
            consts, quads = (ident, ident16, mask16), (qs, ks, vq, loaded)
            project(nc, x, w_qkv, qk_parts, v_rows, consts, quads)
            attend(nc, qk_parts, v_rows, division, consts, quads, load_weights, load_in)
        feed(nc, division, (x_in, a_in, in_loaded), load_in, (w1_sb, w2_sb, wo2_sb, bias, mixk, wout_sb, row), w_loaded, out)


def kernel(**inputs):
    import numpy as _np
    import concourse.bacc as _bacc
    from concourse import mybir as _mybir
    from concourse.bass_utils import run_bass_kernel_spmd as _run

    nc = _bacc.Bacc("TRN2", target_bir_lowering=False, num_devices=1)
    arrays, args = {}, []
    for name in _INS:
        a = _np.ascontiguousarray(inputs[name])
        arrays[f"in_{name}_dram"] = a
        args.append(nc.dram_tensor(f"in_{name}_dram", a.shape, _mybir.dt.from_np(a.dtype), kind="ExternalInput").ap())
    out = nc.dram_tensor("out_0_dram", (BATCH, SEQ, D), F32, kind="ExternalOutput").ap()
    layer(nc, *args, out)
    r = _run(nc, [arrays], core_ids=[0])
    return r.results[0]["out_0_dram"]
```
